# Optimizing a Trainium2 kernel written in Bass

```python
import numpy as np
import jax
import jax.numpy as jnp

def _softmax(x, axis=-1):
    return jax.nn.softmax(x, axis=axis)

def _gelu(x):
    return jax.nn.gelu(x, approximate=True)

def _silu(x):
    return jax.nn.silu(x)

def _sigmoid(x):
    return jax.nn.sigmoid(x)

def _layernorm(x, axis=-1, eps=1e-05):
    m = jnp.mean(x, axis=axis, keepdims=True)
    v = jnp.var(x, axis=axis, keepdims=True)
    return (x - m) / jnp.sqrt(v + eps)

def _scatter_add(tgt, idx, src, axis=0):
    return tgt.at[idx].add(src)

def _segment_sum(src, seg, n):
    return jax.ops.segment_sum(src, seg, n)
kernel_name = 'mk_seq_preln_d1_jaxref_r4_818c5d'

def setup_inputs(seed: int=0):
    np.random.seed(seed)
    _w = jnp.asarray

    def _L0_attn_setup():
        import jax, jax.numpy as jnp
        import numpy as np
        import math
        H = 16
        N_EMBD = 256
        EPS = 1e-05
        key = jax.random.key(seed)
        ks = jax.random.split(key, 6)
        B, T, C = (2, 512, 256)
        x = jax.random.normal(ks[0], (B, T, C), dtype=jnp.float32)
        s = 0.02
        Wq = jax.random.normal(ks[1], (C, N_EMBD), dtype=jnp.float32) * s
        Wk = jax.random.normal(ks[2], (C, N_EMBD), dtype=jnp.float32) * s
        Wv = jax.random.normal(ks[3], (C, N_EMBD), dtype=jnp.float32) * s
        Wo = jax.random.normal(ks[4], (N_EMBD, C), dtype=jnp.float32) * s
        return {'x': x, 'Wq': Wq, 'bq': jnp.zeros((N_EMBD,), jnp.float32), 'Wk': Wk, 'bk': jnp.zeros((N_EMBD,), jnp.float32), 'Wv': Wv, 'bv': jnp.zeros((N_EMBD,), jnp.float32), 'Wo': Wo, 'bo': jnp.zeros((C,), jnp.float32), 'gamma': jnp.ones((C,), jnp.float32), 'beta': jnp.zeros((C,), jnp.float32)}
    _L0_attn_in = _L0_attn_setup()

    def _L0_ffn_setup():
        import jax, jax.numpy as jnp
        import numpy as np
        import math
        D_IN = 256
        FEATURES = (1024, 1024, 256)
        BATCH, SEQ = (8, 512)

        def _conn_dense(kernel_bool, x):
            w = jnp.where(kernel_bool, jnp.float32(1.0), jnp.float32(-1.0))
            return x @ w
        key = jax.random.key(seed)
        kx, kk0, kk1, kk2 = jax.random.split(key, 4)
        x = jax.random.normal(kx, (BATCH, SEQ, D_IN), dtype=jnp.float32)
        k0 = jax.random.randint(kk0, (2 * D_IN, FEATURES[0]), 0, 2).astype(jnp.bool_)
        k1 = jax.random.randint(kk1, (FEATURES[0], FEATURES[1]), 0, 2).astype(jnp.bool_)
        k2 = jax.random.randint(kk2, (FEATURES[1], FEATURES[2]), 0, 2).astype(jnp.bool_)
        s0 = jnp.asarray(1.0 / math.sqrt(2 * D_IN), dtype=jnp.float32)
        s1 = jnp.asarray(1.0 / math.sqrt(FEATURES[0]), dtype=jnp.float32)
        s2 = jnp.asarray(1.0 / math.sqrt(FEATURES[1]), dtype=jnp.float32)
        return {'x': x, 'k0': k0, 'k1': k1, 'k2': k2, 's0': s0, 's1': s1, 's2': s2}
    _L0_ffn_in = _L0_ffn_setup()
    _d = {'L0_attn_x': _L0_attn_in['x'], 'L0_attn_Wq': _L0_attn_in['Wq'], 'L0_attn_bq': _L0_attn_in['bq'], 'L0_attn_Wk': _L0_attn_in['Wk'], 'L0_attn_bk': _L0_attn_in['bk'], 'L0_attn_Wv': _L0_attn_in['Wv'], 'L0_attn_bv': _L0_attn_in['bv'], 'L0_attn_Wo': _L0_attn_in['Wo'], 'L0_attn_bo': _L0_attn_in['bo'], 'L0_attn_gamma': _L0_attn_in['gamma'], 'L0_attn_beta': _L0_attn_in['beta'], 'L0_ffn_k0': _L0_ffn_in['k0'], 'L0_ffn_k1': _L0_ffn_in['k1'], 'L0_ffn_k2': _L0_ffn_in['k2'], 'L0_ffn_s0': _L0_ffn_in['s0'], 'L0_ffn_s1': _L0_ffn_in['s1'], 'L0_ffn_s2': _L0_ffn_in['s2']}
    _x0 = _d['L0_attn_x']
    _d['L0_attn_x'] = jax.random.normal(jax.random.fold_in(jax.random.key(seed), 1), (16, 512, 256), dtype=_x0.dtype)
    del _x0
    return _d

def reference(L0_attn_x, L0_attn_Wq, L0_attn_bq, L0_attn_Wk, L0_attn_bk, L0_attn_Wv, L0_attn_bv, L0_attn_Wo, L0_attn_bo, L0_attn_gamma, L0_attn_beta, L0_ffn_k0, L0_ffn_k1, L0_ffn_k2, L0_ffn_s0, L0_ffn_s1, L0_ffn_s2):

    def _L0_attn_ref(x, Wq, bq, Wk, bk, Wv, bv, Wo, bo, gamma, beta):
        import jax, jax.numpy as jnp
        import numpy as np
        import math
        H = 16
        N_EMBD = 256
        EPS = 1e-05
        B, T, _ = x.shape
        Dh = N_EMBD // H

        def split_heads(y):
            return y.reshape(B, T, H, Dh).transpose(0, 2, 1, 3)
        q = split_heads(x @ Wq + bq)
        k = split_heads(x @ Wk + bk)
        v = split_heads(x @ Wv + bv)
        att = jnp.einsum('bhtd,bhsd->bhts', q, k) * (1.0 / math.sqrt(Dh))
        causal = jnp.tril(jnp.ones((T, T), dtype=bool))
        att = jnp.where(causal[None, None], att, -jnp.inf)
        att = jax.nn.softmax(att, axis=-1)
        o = jnp.einsum('bhts,bhsd->bhtd', att, v)
        o = o.transpose(0, 2, 1, 3).reshape(B, T, N_EMBD)
        y = o @ Wo + bo
        mu = jnp.mean(y, axis=-1, keepdims=True)
        var = jnp.var(y, axis=-1, keepdims=True)
        return (y - mu) * jax.lax.rsqrt(var + EPS) * gamma + beta

    def _L0_ffn_ref(x, k0, k1, k2, s0, s1, s2):
        import jax, jax.numpy as jnp
        import numpy as np
        import math
        D_IN = 256
        FEATURES = (1024, 1024, 256)
        BATCH, SEQ = (8, 512)

        def _conn_dense(kernel_bool, x):
            w = jnp.where(kernel_bool, jnp.float32(1.0), jnp.float32(-1.0))
            return x @ w
        h = jnp.concatenate([x, -x], axis=-1)
        h = s0 * _conn_dense(k0, h)
        h = jax.nn.relu(h) * 2
        h = s1 * _conn_dense(k1, h)
        h = jax.nn.relu(h) * 2
        h = s2 * _conn_dense(k2, h)
        return h
    x = L0_attn_x
    x = x + _L0_attn_ref(_layernorm(x, axis=-1), L0_attn_Wq, L0_attn_bq, L0_attn_Wk, L0_attn_bk, L0_attn_Wv, L0_attn_bv, L0_attn_Wo, L0_attn_bo, L0_attn_gamma, L0_attn_beta)
    x = x + _L0_ffn_ref(_layernorm(x, axis=-1), L0_ffn_k0, L0_ffn_k1, L0_ffn_k2, L0_ffn_s0, L0_ffn_s1, L0_ffn_s2)
    return x

_drawn_inputs = setup_inputs


def setup_inputs(seed=0):
    import zlib

    import numpy as np

    out = dict(_drawn_inputs(seed))
    spreads = {'L0_attn_bq': (0.0, 0.8),
     'L0_attn_bk': (0.0, 0.8),
     'L0_attn_bv': (0.0, 0.1),
     'L0_attn_bo': (0.0, 0.1),
     'L0_attn_gamma': (1.0, 0.2),
     'L0_attn_beta': (0.0, 0.1)}
    factors = {'L0_attn_Wq': 6.756, 'L0_attn_Wk': 6.378}
    for name, (base, spread) in spreads.items():
        noise = np.random.default_rng([zlib.crc32(name.encode()), seed]).standard_normal(out[name].shape)
        drawn = base * np.exp(spread * noise) if base else spread * noise
        out[name] = jnp.asarray(drawn.astype(out[name].dtype))
    for name, factor in factors.items():
        out[name] = (out[name] * factor).astype(out[name].dtype)
    return out
```

```python
import concourse.bass as bass
from concourse import mybir
from contextlib import ExitStack

P = 128


def layer_kernel(nc, x, Wq, bq, Wk, bk, Wv, bv, Wo, bo, gamma, beta, k0, k1, k2, s0, s1, s2, out):
    f32, bf16, f16, u8 = mybir.dt.float32, mybir.dt.bfloat16, mybir.dt.float16, mybir.dt.uint8
    ALU, ACT, AX = mybir.AluOpType, mybir.ActivationFunctionType, mybir.AxisListType

    B, T, C = x.shape
    H = 16
    D = C // H
    F = k1.shape[0]
    EPS = 1e-5
    NT = T // P
    KC = C // P
    KF = F // P
    HT = H // KC
    SLOT_Q = (0, 0, 1, 1, 0, 2)
    SLOT_K = (0, 1, 0, 1, 2, 0)
    ROWS_QK = 16 * len(SLOT_Q)
    ROWS_SHIFT = ROWS_QK + 3
    NS = (H // 2) * NT
    NG = H // 4
    NC_USES = 2 + 2 * KF + 2
    H2_SCALE = 1.0 / 16.0
    LOOP0, LOOP1 = 3, 15

    xv = x.rearrange("b (n p) c -> b p n c", p=P)
    ov = out.rearrange("b (n p) c -> b p n c", p=P)

    ctx = ExitStack()
    with ctx:
        def sb(name, shape, dt):
            return ctx.enter_context(nc.sbuf_tensor(name, shape, dt))

        def sem(name):
            return ctx.enter_context(nc.semaphore(name))

        ident = sb("ident", [P, P], f32)
        identh = sb("identh", [P, P], bf16)
        causal = sb("causal", [P, P], f32)
        wqk = sb("wqk", [P, 4, KC, P], f32)
        wv = sb("wv", [P, KC, C], f32)
        wo = sb("wo", [P, KC, C], f32)
        bqk = sb("bqk", [P, 4], f32)
        rows = sb("rows", [P, 4, C], f32)
        bv_r, bo_r, gamma_r, beta_r = (rows[:, n, :] for n in range(4))
        w0 = sb("w0", [P, KC, F], f16)
        w1 = sb("w1", [P, KF, F], f16)
        w2 = sb("w2", [P, KF, C], f16)
        sc = sb("sc", [P, 16], f32)
        neghalf = sb("neghalf", [P, NT], f32)
        idle_p = sb("idle_p", [P, 2], f32)
        idle_v = sb("idle_v", [P, 2], f32)
        x_in = sb("x_in", [P, NT, C], f32)
        parts = sb("parts", [P, 2, 3, T], bf16)
        resid = sb("resid", [P, T], f32)
        qS = [sb(f"qS{n}", [P, H, T], bf16) for n in range(2)]
        kS = [sb(f"kS{n}", [P, H, T], bf16) for n in range(2)]
        vv = [sb(f"vv{n}", [P, NT, H, 32], f32) for n in range(2)]
        negm = sb("negm", [P, NT, H], f32)
        negr = resid[:, 0:NT * H].rearrange("p (n h) -> p n h", n=NT)
        mparts = sb("mparts", [P, NT, 3 * H], bf16)
        mT = sb("mT", [2 * 3 * H, NT // 2, P], bf16)
        probs = [sb(f"probs{n}", [P, 4, T], f32) for n in range(2)]
        osum = [sb(f"osum{n}", [P, T], f32) for n in range(2)]
        att = sb("att", [P, KC, T], f32)
        sums = sb("sums", [P, KC, T], f32)
        y = sb("y", [P, NT, C], f32)
        x1 = [sb(f"x1_{n}", [P, NT, C], f32) for n in range(2)]
        zT = [sb(f"zT{n}", [P, KC, T], f16) for n in ("h", "l")]
        h1 = [sb(f"h1{n}", [P, KF, T], f16) for n in ("h", "l")]
        h2 = [sb(f"h2{n}", [P, KF, T], f16) for n in ("h", "l")]
        xnT = h1[0][:, 0:2 * KC, :].rearrange("p a t -> p (a t)").bitcast(f32).rearrange("p (k t) -> p k t", k=KC)
        k1_raw = h2[0][:, :, :].rearrange("p a t -> p (a t)").bitcast(u8)[:, 0:KF * F].rearrange("p (k f) -> p k f", k=KF)
        h2l_raw = h2[1][:, :, :].rearrange("p a t -> p (a t)").bitcast(u8)
        k0_raw = h2l_raw[:, 0:2 * KC * F].rearrange("p (k f) -> p k f", k=2 * KC)
        k2_raw = h2l_raw[:, 2 * KC * F:2 * KC * F + KF * C].rearrange("p (k c) -> p k c", k=KF)
        wq_raw = att[:, :, 0:C]
        wk_raw = sums[:, :, 0:C]

        psA = ctx.enter_context(nc.psum_tensor("psA", [P, 2, T], f32))
        psB = ctx.enter_context(nc.psum_tensor("psB", [P, 2, T], f32))
        psV = ctx.enter_context(nc.psum_tensor("psV", [P, T], f32))
        psC = ctx.enter_context(nc.psum_tensor("psC", [P, 3, T], f32))

        s_wts = sem("weights_loaded")
        s_scl = sem("scalars_loaded")
        s_zero = sem("pool_cleared")
        s_const = sem("constants_ready")
        s_wqk = sem("wqk_ready")
        s_sgn = sem("signs_ready")
        s_sgs = sem("signs_steps")
        s_w0d = sem("w0_difference")
        s_wffn = sem("ffn_weights_ready")
        s_x = sem("x_loaded")
        s_xT = sem("xT_in_psum")
        s_xnT = sem("xnT_ready")
        s_qk = sem("qk_in_psum")
        s_hi = sem("qk_high_ready")
        s_r1 = sem("qk_rest_ready")
        s_mid = sem("qk_mid_ready")
        s_lo = sem("qk_low_ready")
        s_stack = [sem(f"stacked{j}") for j in range(4)]
        s_vps = sem("v_in_psum")
        s_v = sem("v_ready")
        s_s = sem("scores_in_psum")
        s_masked = sem("scores_masked")
        s_max = sem("max_taken")
        s_mstep = sem("max_part_steps")
        s_mparts = sem("max_parts_ready")
        s_mTps = sem("maxT_in_psum")
        s_mT = sem("maxT_ready")
        s_shift = sem("shift_rows_loaded")
        s_st = sem("scoresT_in_psum")
        s_exp = sem("exp_done")
        s_tri = sem("probs_masked")
        s_pv = sem("pv_done")
        s_o = sem("pv_copied")
        s_pack = [sem(f"packed{n}") for n in range(2)]
        s_rec = sem("sums_inverted")
        s_att = sem("attention_divided")
        s_res = sem("residual_loaded")
        s_xb = sem("residual_plus_beta")
        s_wo = sem("wo_in_psum")
        s_y = sem("y_ready")
        s_yg = sem("y_times_gamma")
        s_x1 = sem("x1_ready")
        s_c = sem("ffn_in_psum")
        s_ch = sem("ffn_high_ready")
        s_cl = sem("ffn_bank_read")
        s_out = sem("out_stored")

        class Norm:
            def __init__(self, tag):
                self.stats = sb(f"stats_{tag}", [P, NT, 6], f32)
                self.mv = sb(f"mv_{tag}", [P, NT, 2], f32)
                self.ve = sb(f"ve_{tag}", [P, NT], f32)
                self.rstd = sb(f"rstd_{tag}", [P, NT], f32)
                self.s_stats, self.s_mv, self.s_ve, self.s_rstd, self.s_out = (
                    sem(f"{tag}_{w}") for w in ("stats", "mean_var", "var_eps", "rstd", "normed"))

        ln1, lny, ln2 = Norm("ln1"), Norm("lny"), Norm("ln2")
        block = ctx.enter_context(nc.Block())

        def past(row, first=0):
            return not isinstance(row, int) or row > first

        def run(eng, iteration):
            for i in range(LOOP0):
                iteration(i, i % 2)
            with eng.Fori(LOOP0, LOOP1 - 1, 2) as i:
                iteration(i, LOOP0 % 2, True)
                iteration(i + 1, (LOOP0 + 1) % 2, True)
            for i in range(LOOP1, B + 3):
                iteration(i, i % 2)

        def stages(i, looped):
            def row(n):
                return n if looped or 0 <= n < B else None
            return row(i), row(i - 1), row(i - 2), row(i - 3), row(i + 1)

        FIRST_S = 4
        def s_units(s):
            def upto(n):
                return 0 if n < FIRST_S else -(-(n - FIRST_S + 1) * NS // (NS - FIRST_S))
            return range(upto(s - 1), upto(s))

        def c_bank(u):
            return psC[:, u % 3, :]

        @block.sync
        def _(sp):
            sp.dma_start(x_in[:, :, :], xv[0]).then_inc(s_x, 16)
            sp.dma_start(wq_raw, Wq.rearrange("(k p) n -> p k n", p=P)).then_inc(s_wts, 16)
            sp.dma_start(wk_raw, Wk.rearrange("(k p) n -> p k n", p=P)).then_inc(s_wts, 16)
            sp.dma_start(wv[:, :, :], Wv.rearrange("(k p) n -> p k n", p=P)).then_inc(s_wts, 16)
            with nc.allow_non_contiguous_dma(reason="biases to partitions in (d, head) order"):
                for j in range(4):
                    b = (bq, bk)[j % 2]
                    src = b[(j // 2) * P:(j // 2 + 1) * P].rearrange("(h d o) -> d h o", d=D, o=1)
                    sp.dma_start(bqk[:, j:j + 1], src).then_inc(s_wts, 16)
            for n, r in enumerate((bv, bo, gamma, beta)):
                sp.dma_start(rows[:, n, :], r.partition_broadcast(P)).then_inc(s_wts, 16)
            for n, s in enumerate((s0, s1, s2)):
                sp.dma_start(sc[:, n:n + 1], s.partition_broadcast(P)).then_inc(s_scl, 16)
            sp.dma_start(k0_raw, k0.rearrange("(k p) f -> p k f", p=P)).then_inc(s_scl, 16)
            sp.dma_start(k1_raw, k1.rearrange("(k p) f -> p k f", p=P)).then_inc(s_scl, 16)
            sp.dma_start(k2_raw, k2.rearrange("(k p) c -> p k c", p=P)).then_inc(s_scl, 16)
            sp.dma_start(wo[:, :, :], Wo.rearrange("(k p) n -> p k n", p=P)).then_inc(s_wts, 16)

            def stack(a, par, j):
                t, dst = j // 2, (qS, kS)[j % 2][par]
                for n, part in enumerate((SLOT_Q, SLOT_K)[j % 2]):
                    if n == 0:
                        sp.wait_ge(s_hi, 4 * a + j + 1)
                        sp.wait_ge(s_lo, 4 * a + j + 1)
                    sp.dma_start(dst[16 * n:16 * n + 16, HT * t:HT * t + HT, :],
                                 parts[:, j % 2, part, :]).then_inc(s_stack[j], 16)

            def pack(b, g):
                sp.wait_ge(s_o, NG * b + g + 1)
                t, r0 = g // 2, (g % 2) * 64
                for i4 in range(4):
                    r = r0 + 16 * i4
                    sp.dma_start(att[r:r + 16, t, :], osum[g % 2][32 * i4:32 * i4 + 16, :]).then_inc(s_pack[g % 2], 16)
                    sp.dma_start(sums[r:r + 16, t, :], osum[g % 2][32 * i4 + 16:32 * i4 + 32, :]).then_inc(s_pack[g % 2], 16)

            def store(c, par, n):
                sp.wait_ge(s_cl, NC_USES * c + NC_USES - 1 + n)
                sp.dma_start(ov[c][:, 2 * n:2 * n + 2, :], x1[par][:, 2 * n:2 * n + 2, :]).then_inc(s_out, 16)

            def iteration(i, par, looped=False):
                a, b, c, cr, an = stages(i, looped)
                if a is not None:
                    for j in range(4):
                        stack(a, par, j)
                if b is not None:
                    sp.wait_ge(s_mT, b + 1)
                    dst = qS[1 - par][ROWS_QK:ROWS_SHIFT, :, :].rearrange("r h (n e q) -> r e h n q", e=2, q=P)
                    for e in range(2):
                        sp.dma_start(dst[:, e], mT[3 * H * e:3 * H * (e + 1), :, :]).then_inc(s_shift, 16)
                if cr is not None:
                    store(cr, 1 - par, 1)
                if b is not None:
                    if past(b, 1):
                        sp.wait_ge(s_out, 32 * (b - 1))
                    sp.dma_start(x1[1 - par][:, :, :], xv[b]).then_inc(s_res, 16)
                if an is not None:
                    sp.wait_ge(s_xT, 2 * an)
                    sp.dma_start(x_in[:, :, :], xv[an]).then_inc(s_x, 16)
                if b is not None:
                    for g in range(NG):
                        pack(b, g)
                if c is not None:
                    store(c, par, 0)

            run(sp, iteration)
            sp.wait_ge(s_out, 32 * B)

        @block.gpsimd
        def _(pool):
            pool.memset(ident[:, :], 0.0)
            pool.memset(identh[:, :], 0.0)
            pool.memset(causal[:, :], 0.0)
            pool.memset(idle_p[:, :], 0.0)
            pool.memset(neghalf[:, :], -0.5).then_inc(s_zero, 1)
            pool.wait_ge(s_zero, 1)
            for m in (ident, identh):
                pool.affine_select(out=m[:, :], in_=m[:, :], compare_op=ALU.not_equal, fill=1.0, base=0,
                                   pattern=[[-1, P]], channel_multiplier=1)
            pool.affine_select(out=causal[:, :], in_=causal[:, :], compare_op=ALU.is_ge, fill=-3.0e38, base=0,
                               pattern=[[-1, P]], channel_multiplier=1).then_inc(s_const, 1)

            def rstd(ln, row):
                pool.wait_ge(ln.s_ve, row + 1)
                pool.tensor_tensor(ln.rstd[:, :], ln.ve[:, :], neghalf[:, :], ALU.pow).then_inc(ln.s_rstd, 1)

            rstd(ln1, 0)
            pool.wait_ge(s_scl, 16 * 6)
            pool.wait_ge(s_sgn, 1)
            for k in range(KF):
                pool.tensor_scalar(w1[:, k, :], k1_raw[:, k, :], sc[:, 5:6], sc[:, 6:7], ALU.mult, ALU.add)
            pool.tensor_scalar(w2[:, :, :], k2_raw, 2.0, -1.0, ALU.mult, ALU.add).then_inc(s_wffn, 1)

            def triangle(b, s):
                j, pr = s // 2, s % 2
                pool.wait_ge(s_exp, NS * b + s + 1)
                if past(b) or s > 0:
                    pool.wait_ge(s_tri, NS * b + s)
                pool.tensor_tensor(idle_p[:, 0:1], idle_p[:, 1:2], idle_p[:, 1:2], ALU.add)
                p = probs[j % 2][:, 2 * pr:2 * pr + 2, 0:P]
                pool.affine_select(out=p, in_=p, compare_op=ALU.is_ge, fill=0.0, base=0,
                                   pattern=[[0, 2], [1, P]], channel_multiplier=-1).then_inc(s_tri, 1)

            def iteration(i, par, looped=False):
                a, b, c, cr, an = stages(i, looped)
                if c is not None:
                    rstd(lny, c)
                    rstd(ln2, c)
                if b is not None:
                    pool.wait_ge(s_res, 16 * (b + 1))
                    pool.tensor_tensor(x1[1 - par][:, :, :], x1[1 - par][:, :, :],
                                       beta_r[:, None, :].to_broadcast([P, NT, C]), ALU.add).then_inc(s_xb, 1)
                for s in range(NS):
                    if b is not None:
                        triangle(b, s)
                    if s == 10 and an is not None:
                        rstd(ln1, an)

            run(pool, iteration)

        @block.scalar
        def _(act):
            act.wait_ge(s_wts, 16 * 12)

            def qk_high(a, j):
                act.wait_ge(s_qk, 4 * a + j + 1)
                if j >= 2:
                    act.wait_ge(s_stack[j - 2], 96 * (a + 1))
                elif past(a):
                    act.wait_ge(s_stack[j + 2], 96 * a)
                act.activation(parts[:, j % 2, 0, :], psA[:, j % 2, :], ACT.Identity,
                               bias=bqk[:, j:j + 1]).then_inc(s_hi, 1)

            def ffn_high(c, u):
                act.wait_ge(s_c, NC_USES * c + u + 1)
                if u < 2:
                    act.activation(zT[0][:, u, :], c_bank(u), ACT.Copy).then_inc(s_ch, 1)
                else:
                    h = (h1 if u < 2 + KF else h2)[0]
                    act.activation(h[:, (u - 2) % KF, :], c_bank(u), ACT.Relu).then_inc(s_ch, 1)

            def exp(b, s):
                g, kb, pr = s // 8, (s % 8) // 2, s % 2
                j, n = s // 2, T - P * kb
                act.wait_ge(s_st, NS * b + s + 1)
                if past(b) or j > 1:
                    act.wait_ge(s_pv, (NS // 2) * b + j - 1)
                act.activation(probs[j % 2][:, 2 * pr:2 * pr + 2, 0:n], psB[:, :, 0:n], ACT.Exp,
                               scale=D ** -0.5).then_inc(s_exp, 1)

            def pv_copy(b, g):
                act.wait_ge(s_pv, (NS // 2) * b + 4 * g + 4)
                if past(b) or g > 1:
                    act.wait_ge(s_pack[g % 2], 128 * (2 * b + g // 2))
                act.activation(osum[g % 2][:, :], psV[:, :], ACT.Copy).then_inc(s_o, 1)

            def iteration(i, par, looped=False):
                a, b, c, cr, an = stages(i, looped)
                if a is not None:
                    for k in range(KC):
                        act.wait_ge(s_xT, 2 * a + k + 1)
                        act.activation(xnT[:, k, :], psA[:, k, :], ACT.Copy).then_inc(s_xnT, 1)
                    for j in range(4):
                        qk_high(a, j)
                if b is not None:
                    act.wait_ge(s_mTps, b + 1)
                    if past(b):
                        act.wait_ge(s_shift, 32 * b)
                    act.activation(mT[:, :, :].rearrange("r n q -> r (n q)"),
                                   psB[0:2 * 3 * H, 0, :].bitcast(bf16)[:, 0:T // 2], ACT.Copy).then_inc(s_mT, 1)
                if c is not None:
                    for u in range(2 + KF):
                        ffn_high(c, u)
                for s in range(NS):
                    if c is not None and s % 4 == 0 and s > 0:
                        ffn_high(c, 2 + KF + s // 4 - 1)
                    if b is not None:
                        exp(b, s)
                        if s % 8 == 2 and s > 8:
                            pv_copy(b, s // 8 - 1)
                if c is not None:
                    ffn_high(c, 2 + 2 * KF - 1)
                if b is not None:
                    pv_copy(b, NG - 1)

            run(act, iteration)

        @block.vector
        def _(dve):
            def norm_stats(ln, row, src):
                for n in range(NT):
                    last = dve.bn_stats(ln.stats[:, n, :], src[:, n, :])
                last.then_inc(ln.s_stats, 1)
                dve.wait_ge(ln.s_stats, row + 1)
                dve.tensor_copy(idle_v[:, 0:1], idle_v[:, 1:2])
                for n in range(NT):
                    last = dve.bn_aggr(ln.mv[:, n, :], ln.stats[:, n, :])
                last.then_inc(ln.s_mv, 1)
                dve.wait_ge(ln.s_mv, row + 1)
                dve.tensor_scalar(ln.ve[:, :], ln.mv[:, :, 1], EPS, None, ALU.add).then_inc(ln.s_ve, 1)

            def norm_apply(ln, row, dst, src):
                dve.wait_ge(ln.s_rstd, row + 1)
                for n in range(NT):
                    last = dve.tensor_scalar(dst[:, n, :], src[:, n, :], ln.mv[:, n, 0:1], ln.rstd[:, n:n + 1],
                                             ALU.subtract, ALU.mult)
                last.then_inc(ln.s_out, 1)

            dve.memset(idle_v[:, :], 0.0)
            dve.wait_ge(s_x, 16)
            dve.wait_ge(s_const, 1)
            norm_stats(ln1, 0, x_in)
            dve.wait_ge(s_wts, 16 * 12)
            for j in range(4):
                raw = (wq_raw, wk_raw)[j % 2]
                for k in range(KC):
                    last = dve.tensor_copy(
                        wqk[:, j, k, :].rearrange("p (d h) -> p d h", h=HT),
                        raw[:, k, (j // 2) * P:(j // 2 + 1) * P].rearrange("p (h d) -> p d h", d=D))
            last.then_inc(s_wqk, 1)
            norm_apply(ln1, 0, x_in, x_in)
            for n in range(2):
                dve.memset(vv[n][:, :, :, D:2 * D], 1.0)
                dve.memset(kS[n][ROWS_QK:ROWS_SHIFT, :, :], 1.0)
            dve.wait_ge(s_scl, 16 * 6)
            steps = [0]

            def step(ins):
                steps[0] += 1
                ins.then_inc(s_sgs, 1)
                dve.wait_ge(s_sgs, steps[0])

            step(dve.tensor_scalar(sc[:, 8:10], sc[:, 0:2], 0.0, None, ALU.is_gt))
            step(dve.tensor_scalar(sc[:, 10:12], sc[:, 0:2], 0.0, None, ALU.is_lt))
            step(dve.tensor_tensor(sc[:, 12:14], sc[:, 8:10], sc[:, 10:12], ALU.subtract))
            step(dve.tensor_scalar(sc[:, 3:4], sc[:, 12:13], 2.0, None, ALU.mult))
            step(dve.tensor_scalar(sc[:, 5:6], sc[:, 13:14], 2.0 * H2_SCALE, None, ALU.mult))
            dve.tensor_scalar(sc[:, 6:7], sc[:, 13:14], -H2_SCALE, None, ALU.mult).then_inc(s_sgn, 1)
            step(dve.tensor_tensor(sc[:, 14:16], sc[:, 0:2], sc[:, 12:14], ALU.mult))
            step(dve.tensor_tensor(sc[:, 8:9], sc[:, 14:15], sc[:, 15:16], ALU.mult))
            step(dve.tensor_tensor(sc[:, 9:10], sc[:, 8:9], sc[:, 2:3], ALU.mult))
            step(dve.tensor_scalar(sc[:, 7:8], sc[:, 9:10], 4.0 / H2_SCALE, None, ALU.mult))
            for k in range(KC):
                last = dve.tensor_tensor(w0[:, k, :], k0_raw[:, k, :], k0_raw[:, KC + k, :], ALU.subtract)
            last.then_inc(s_w0d, 1)
            dve.wait_ge(s_w0d, 1)
            dve.tensor_scalar(w0[:, :, :], w0[:, :, :], sc[:, 3:4], None, ALU.mult).then_inc(s_wffn, 1)

            def qk_parts(a, j):
                bank, p = psA[:, j % 2, :], parts[:, j % 2]
                if past(a) or j > 0:
                    dve.wait_ge(s_lo, 4 * a + j)
                if j == 0 and past(a):
                    dve.wait_ge(s_mparts, a)
                dve.wait_ge(s_hi, 4 * a + j + 1)
                dve.scalar_tensor_tensor(out=resid[:, :], in0=bank, scalar=bqk[:, j:j + 1], in1=p[:, 0, :],
                                         op0=ALU.add, op1=ALU.subtract).then_inc(s_r1, 1)
                dve.wait_ge(s_r1, 4 * a + j + 1)
                dve.tensor_copy(p[:, 1, :], resid[:, :]).then_inc(s_mid, 1)
                dve.wait_ge(s_mid, 4 * a + j + 1)
                dve.tensor_tensor(p[:, 2, :], resid[:, :], p[:, 1, :], ALU.subtract).then_inc(s_lo, 1)

            def v_copy(a, par, n):
                dve.wait_ge(s_vps, 2 * a + n + 1)
                for e in range(2):
                    last = dve.tensor_tensor(
                        vv[par][:, 2 * n + e, :, 0:D],
                        psA[:, n, e * C:(e + 1) * C].rearrange("p (h d) -> p h d", d=D),
                        bv_r.rearrange("p (h d) -> p h d", d=D), ALU.add)
                last.then_inc(s_v, 1)

            def unit_max(a, u):
                hp, qb = u // NT, u % NT
                dve.wait_ge(s_s, NS * a + u + 1)
                diag = psA[:, :, qb * P:(qb + 1) * P]
                dve.tensor_tensor(diag, diag, causal[:, None, :].to_broadcast([P, 2, P]), ALU.add).then_inc(s_masked, 1)
                dve.wait_ge(s_masked, NS * a + u + 1)
                dve.tensor_reduce(negm[:, qb, 2 * hp:2 * hp + 2], psA[:, :, 0:(qb + 1) * P], axis=AX.X,
                                  op=ALU.max, negate=True).then_inc(s_max, 1)

            def max_parts(a):
                dve.wait_ge(s_max, NS * (a + 1))
                if past(a):
                    dve.wait_ge(s_mTps, a)
                part = [mparts[:, :, H * n:H * n + H] for n in range(3)]
                dve.tensor_copy(part[0], negm[:, :, :]).then_inc(s_mstep, 1)
                dve.wait_ge(s_mstep, 3 * a + 1)
                dve.tensor_tensor(negr[:, :, :], negm[:, :, :], part[0], ALU.subtract).then_inc(s_mstep, 1)
                dve.wait_ge(s_mstep, 3 * a + 2)
                dve.tensor_copy(part[1], negr[:, :, :]).then_inc(s_mstep, 1)
                dve.wait_ge(s_mstep, 3 * a + 3)
                dve.tensor_tensor(part[2], negr[:, :, :], part[1], ALU.subtract).then_inc(s_mparts, 1)

            def divide(b, t):
                dve.wait_ge(s_pack[0], 128 * (2 * b + t + 1))
                dve.wait_ge(s_pack[1], 128 * (2 * b + t + 1))
                dve.reciprocal(sums[:, t, :], sums[:, t, :]).then_inc(s_rec, 1)
                dve.wait_ge(s_rec, KC * b + t + 1)
                dve.tensor_tensor(att[:, t, :], att[:, t, :], sums[:, t, :], ALU.mult).then_inc(s_att, 1)

            def ffn_low(c, u):
                dve.wait_ge(s_ch, (NC_USES - 2) * c + u + 1)
                if u < 2:
                    dve.tensor_tensor(zT[1][:, u, :], c_bank(u), zT[0][:, u, :], ALU.subtract).then_inc(s_cl, 1)
                else:
                    h, m = (h1 if u < 2 + KF else h2), (u - 2) % KF
                    dve.scalar_tensor_tensor(out=h[1][:, m, :], in0=c_bank(u), scalar=0.0, in1=h[0][:, m, :],
                                             op0=ALU.max, op1=ALU.subtract).then_inc(s_cl, 1)

            def finish(c, par, n):
                u = NC_USES - 2 + n
                dve.wait_ge(s_c, NC_USES * c + u + 1)
                o = x1[par][:, 2 * n:2 * n + 2, :].rearrange("p n c -> p (n c)")
                dve.scalar_tensor_tensor(out=o, in0=c_bank(u), scalar=sc[:, 7:8], in1=o,
                                         op0=ALU.mult, op1=ALU.add).then_inc(s_cl, 1)

            def iteration(i, par, looped=False):
                a, b, c, cr, an = stages(i, looped)
                if a is not None:
                    for j in range(4):
                        qk_parts(a, j)
                if c is not None:
                    for n in range(2):
                        dve.wait_ge(s_wo, 2 * c + n + 1)
                        dve.tensor_tensor(y[:, 2 * n:2 * n + 2, :],
                                          psB[:, n, :].rearrange("p (n c) -> p n c", n=2),
                                          bo_r[:, None, :].to_broadcast([P, 2, C]), ALU.add).then_inc(s_y, 1)
                    dve.wait_ge(s_y, 2 * c + 2)
                    norm_stats(lny, c, y)
                if a is not None:
                    for n in range(2):
                        v_copy(a, par, n)
                if c is not None:
                    norm_apply(lny, c, y, y)
                    dve.wait_ge(lny.s_out, c + 1)
                    dve.tensor_tensor(y[:, :, :], y[:, :, :], gamma_r[:, None, :].to_broadcast([P, NT, C]),
                                      ALU.mult).then_inc(s_yg, 1)
                    dve.wait_ge(s_yg, c + 1)
                    dve.wait_ge(s_xb, c + 1)
                    dve.tensor_tensor(x1[par][:, :, :], x1[par][:, :, :], y[:, :, :], ALU.add).then_inc(s_x1, 1)
                    dve.wait_ge(s_x1, c + 1)
                    norm_stats(ln2, c, x1[par])
                if cr is not None:
                    finish(cr, 1 - par, 1)
                if c is not None:
                    norm_apply(ln2, c, y, x1[par])
                    for u in range(2 + KF):
                        ffn_low(c, u)
                for s in range(NS):
                    if c is not None and s % 4 == 0 and s > 0:
                        ffn_low(c, 2 + KF + s // 4 - 1)
                    if a is not None:
                        for u in s_units(s):
                            unit_max(a, u)
                    if an is not None and s == 8:
                        dve.wait_ge(s_x, 16 * (an + 1))
                        norm_stats(ln1, an, x_in)
                    if an is not None and s == 12:
                        norm_apply(ln1, an, x_in, x_in)
                    if b is not None and s == 22:
                        divide(b, 0)
                if c is not None:
                    ffn_low(c, 2 + 2 * KF - 1)
                if a is not None:
                    max_parts(a)
                if c is not None:
                    finish(c, par, 0)
                if b is not None:
                    divide(b, 1)

            run(dve, iteration)

        @block.tensor
        def _(pe):
            pe.wait_ge(s_const, 1)
            pe.wait_ge(s_wqk, 1)
            pe.wait_ge(s_wts, 16 * 12)

            def x_transposed(a):
                pe.wait_ge(ln1.s_out, a + 1)
                if past(a):
                    pe.wait_ge(s_max, NS * a)
                for k in range(KC):
                    for n in range(NT):
                        last = pe.transpose(psA[:, k, n * P:(n + 1) * P], x_in[:, n, k * P:(k + 1) * P], ident[:, :])
                    last.then_inc(s_xT, 1)

            def qk(a, j):
                if j == 0:
                    pe.wait_ge(s_xnT, 2 * a + 2)
                if j >= 2:
                    pe.wait_ge(s_r1, 4 * a + j - 1)
                for k in range(KC):
                    last = pe.matmul(psA[:, j % 2, :], wqk[:, j, k, :], xnT[:, k, :], start=(k == 0), stop=(k == KC - 1))
                last.then_inc(s_qk, 1)

            def v(a, n):
                pe.wait_ge(s_r1, 4 * a + 3 + n)
                for e in range(2):
                    t = 2 * n + e
                    for k in range(KC):
                        last = pe.matmul(psA[:, n, e * C:(e + 1) * C], xnT[:, k, t * P:(t + 1) * P], wv[:, k, :],
                                         start=(k == 0), stop=(k == KC - 1))
                last.then_inc(s_vps, 1)

            def scores(a, par, u):
                hp, qb = u // NT, u % NT
                if u % (NS // 2) == 0:
                    for j in range(2):
                        pe.wait_ge(s_stack[2 * (u // (NS // 2)) + j], 96 * (a + 1))
                if u == 0:
                    pe.wait_ge(s_v, 2 * a + 2)
                if past(a) or u > 0:
                    pe.wait_ge(s_max, NS * a + u)
                for e in range(2):
                    h, n = 2 * hp + e, (qb + 1) * P
                    last = pe.matmul(psA[:, e, 0:n], qS[par][0:ROWS_QK, h, qb * P:(qb + 1) * P],
                                     kS[par][0:ROWS_QK, h, 0:n], start=True, stop=True)
                last.then_inc(s_s, 1)

            def max_transposed(b):
                pe.wait_ge(s_mparts, b + 1)
                if past(b):
                    pe.wait_ge(s_y, 2 * b)
                if past(b):
                    pe.wait_ge(s_exp, NS * b)
                o = psB[0:2 * 3 * H, 0, :].bitcast(bf16)
                for n in range(NT // 2):
                    last = pe.transpose(o[:, n * P:(n + 1) * P],
                                        mparts[:, 2 * n:2 * n + 2, :].rearrange("q e m -> q (e m)"), identh[:, :])
                last.then_inc(s_mTps, 1)

            def scores_t(b, par, s):
                g, kb, pr = s // 8, (s % 8) // 2, s % 2
                if s == 0:
                    pe.wait_ge(s_shift, 32 * (b + 1))
                if past(b) or s > 0:
                    pe.wait_ge(s_exp, NS * b + s)
                if s == 0:
                    pe.wait_ge(s_mT, b + 1)
                for e in range(2):
                    h = 4 * g + 2 * pr + e
                    last = pe.matmul(psB[:, e, 0:T - kb * P], kS[par][0:ROWS_SHIFT, h, kb * P:(kb + 1) * P],
                                     qS[par][0:ROWS_SHIFT, h, kb * P:T], start=True, stop=True)
                last.then_inc(s_st, 1)

            def pv(b, par, j):
                g, kb = j // NT, j % NT
                pe.wait_ge(s_tri, NS * b + 2 * j + 2)
                if kb == 0:
                    if past(b) or g > 0:
                        pe.wait_ge(s_o, NG * b + g)
                for i4 in range(4):
                    last = pe.matmul(psV[32 * i4:32 * i4 + 32, kb * P:T], vv[par][:, kb, 4 * g + i4, :],
                                     probs[j % 2][:, i4, 0:T - kb * P], start=(kb == 0), stop=(kb == NT - 1))
                last.then_inc(s_pv, 1)

            def project(c):
                pe.wait_ge(s_att, KC * (c + 1))
                pe.wait_ge(s_exp, NS * (c + 1))
                for n in range(NT):
                    for t in range(KC):
                        last = pe.matmul(psB[:, n // 2, (n % 2) * C:(n % 2 + 1) * C], att[:, t, n * P:(n + 1) * P],
                                         wo[:, t, :], start=(t == 0), stop=(t == KC - 1))
                    if n % 2:
                        last.then_inc(s_wo, 1)

            def c_free(c, u):
                if past(c) or u > 2:
                    pe.wait_ge(s_cl, NC_USES * c + u - 2)

            def z_transposed(c):
                pe.wait_ge(ln2.s_out, c + 1)
                for u in range(KC):
                    c_free(c, u)
                    for n in range(NT):
                        last = pe.transpose(c_bank(u)[:, n * P:(n + 1) * P], y[:, n, u * P:(u + 1) * P], ident[:, :])
                    last.then_inc(s_c, 1)

            def ffn1(c, m):
                c_free(c, 2 + m)
                if m == 0:
                    pe.wait_ge(s_cl, NC_USES * c + 2)
                for n, (k, part) in enumerate((k, part) for k in range(KC) for part in range(2)):
                    last = pe.matmul(c_bank(2 + m), w0[:, k, m * P:(m + 1) * P], zT[part][:, k, :],
                                     start=(n == 0), stop=(n == 2 * KC - 1))
                last.then_inc(s_c, 1)

            def ffn2(c, m, k):
                if k == 0:
                    c_free(c, 2 + KF + m)
                if m == 0:
                    pe.wait_ge(s_cl, NC_USES * c + 2 + k + 2)
                for n, (kk, part) in enumerate((kk, part) for kk in (k, k + 1) for part in range(2)):
                    last = pe.matmul(c_bank(2 + KF + m), w1[:, kk, m * P:(m + 1) * P], h1[part][:, kk, :],
                                     start=(k == 0 and n == 0), stop=(k == KF - 2 and n == 3))
                if k == KF - 2:
                    last.then_inc(s_c, 1)

            def ffn3(c, n):
                u = NC_USES - 2 + n
                c_free(c, u)
                pe.wait_ge(s_cl, NC_USES * c + 2 + 2 * KF)
                for e in range(2):
                    t = 2 * n + e
                    for q, (k, part) in enumerate((k, part) for k in range(KF) for part in range(2)):
                        last = pe.matmul(c_bank(u)[:, e * C:(e + 1) * C], h2[part][:, k, t * P:(t + 1) * P], w2[:, k, :],
                                         start=(q == 0), stop=(q == 2 * KF - 1))
                last.then_inc(s_c, 1)

            def iteration(i, par, looped=False):
                a, b, c, cr, an = stages(i, looped)
                if a is not None:
                    x_transposed(a)
                    for j in range(4):
                        qk(a, j)
                if c is not None:
                    project(c)
                if b is not None:
                    max_transposed(b)
                if a is not None:
                    v(a, 0)
                    v(a, 1)
                if cr is not None:
                    ffn3(cr, 1)
                if c is not None:
                    if not looped and c == 0:
                        pe.wait_ge(s_wffn, 2)
                    z_transposed(c)
                    for m in range(KF):
                        ffn1(c, m)
                for s in range(NS):
                    if b is not None:
                        scores_t(b, 1 - par, s)
                        if s % 2 and s >= 3:
                            pv(b, 1 - par, (s - 3) // 2)
                    if a is not None:
                        for u in s_units(s):
                            scores(a, par, u)
                    if c is not None:
                        ffn2(c, s // 4, 2 * (s % 4))
                if b is not None:
                    pv(b, 1 - par, NS // 2 - 1)
                if c is not None:
                    ffn3(c, 0)

            run(pe, iteration)


_INS = ["L0_attn_x", "L0_attn_Wq", "L0_attn_bq", "L0_attn_Wk", "L0_attn_bk", "L0_attn_Wv", "L0_attn_bv",
        "L0_attn_Wo", "L0_attn_bo", "L0_attn_gamma", "L0_attn_beta", "L0_ffn_k0", "L0_ffn_k1", "L0_ffn_k2",
        "L0_ffn_s0", "L0_ffn_s1", "L0_ffn_s2"]


def kernel(**inputs):
    import numpy as np
    import concourse.bacc as bacc
    from concourse.bass_utils import run_bass_kernel_spmd

    nc = bacc.Bacc("TRN2", target_bir_lowering=False, num_devices=1)
    arrays, args = {}, []
    for name in _INS:
        a = np.ascontiguousarray(inputs[name])
        a = a.reshape(a.shape or (1,))
        arrays[f"in_{name}"] = a
        args.append(nc.dram_tensor(f"in_{name}", a.shape, mybir.dt.from_np(a.dtype), kind="ExternalInput").ap())
    shape = tuple(inputs["L0_attn_x"].shape)
    args.append(nc.dram_tensor("out_0", shape, mybir.dt.float32, kind="ExternalOutput").ap())
    layer_kernel(nc, *args)
    r = run_bass_kernel_spmd(nc, [arrays], core_ids=[0])
    return r.results[0]["out_0"]
```

```python
import concourse.bass as bass
from concourse import mybir
from contextlib import ExitStack

P = 128


def layer_kernel(nc, x, Wq, bq, Wk, bk, Wv, bv, Wo, bo, gamma, beta, k0, k1, k2, s0, s1, s2, out):
    f32, bf16, f16, u8 = mybir.dt.float32, mybir.dt.bfloat16, mybir.dt.float16, mybir.dt.uint8
    ALU, ACT, AX = mybir.AluOpType, mybir.ActivationFunctionType, mybir.AxisListType

    B, T, C = x.shape
    H = 16
    D = C // H
    F = k1.shape[0]
    EPS = 1e-5
    NT = T // P
    KC = C // P
    KF = F // P
    HT = H // KC
    SLOT_Q = (0, 0, 1, 1, 0, 2)
    SLOT_K = (0, 1, 0, 1, 2, 0)
    ROWS_QK = 16 * len(SLOT_Q)
    ROWS_SHIFT = ROWS_QK + 3
    NU = H * NT
    NS = (H // 2) * NT
    NG = H // 4
    NC_USES = 2 + 2 * KF + 2
    H2_SCALE = 1.0 / 16.0
    LOOP0, LOOP1 = 3, 15

    xv = x.rearrange("b (n p) c -> b p n c", p=P)
    ov = out.rearrange("b (n p) c -> b p n c", p=P)

    ctx = ExitStack()
    with ctx:
        def place(h):
            return (h % HT) * KC + h // HT

        def sb(name, shape, dt):
            return ctx.enter_context(nc.sbuf_tensor(name, shape, dt))

        def sem(name):
            return ctx.enter_context(nc.semaphore(name))

        ident = sb("ident", [P, P], f32)
        identh = sb("identh", [P, P], bf16)
        causal = sb("causal", [P, T], bf16)
        wqk = sb("wqk", [P, 4, KC, P], f32)
        wv = sb("wv", [P, KC, C], f32)
        wo = sb("wo", [P, KC, C], f32)
        bqk = sb("bqk", [P, 4], f32)
        rows = sb("rows", [P, 4, C], f32)
        bv_r, bo_r, gamma_r, beta_r = (rows[:, n, :] for n in range(4))
        w0 = sb("w0", [P, KC, F], f16)
        w1 = sb("w1", [P, KF, F], f16)
        w2 = sb("w2", [P, KF, C], f16)
        sc = sb("sc", [P, 16], f32)
        neghalf = sb("neghalf", [P, NT], f32)
        x_in = sb("x_in", [P, NT, C], f32)
        resid = sb("resid", [P, T], f32)
        qS = [sb(f"qS{n}", [P, H, T], bf16) for n in range(2)]
        kS = [sb(f"kS{n}", [P, H, T], bf16) for n in range(2)]
        vv = [sb(f"vv{n}", [P, NT, H, D, 2], f32) for n in range(2)]
        rowmax = sb("rowmax", [P, NT, H], f32)
        negr = resid[:, 0:NT * H].rearrange("p (n h) -> p n h", n=NT)
        mparts = sb("mparts", [P, NT, 3 * H], bf16)
        mT = sb("mT", [2 * 3 * H, NT // 2, P], bf16)
        probs = [sb(f"probs{n}", [P, 4, T], f32) for n in range(2)]
        osum = [sb(f"osum{n}", [P, T], f32) for n in range(2)]
        asum = sb("asum", [P, 2, KC, T], f32)
        att, sums = asum[:, 0], asum[:, 1]
        y = sb("y", [P, NT, C], f32)
        x1 = [sb(f"x1_{n}", [P, NT, C], f32) for n in range(2)]
        zT = [sb(f"zT{n}", [P, KC, T], f16) for n in ("h", "l")]
        h1 = [sb(f"h1{n}", [P, KF, T], f16) for n in ("h", "l")]
        h2 = [sb(f"h2{n}", [P, KF, T], f16) for n in ("h", "l")]
        xnT = h1[0][:, 0:2 * KC, :].rearrange("p a t -> p (a t)").bitcast(f32).rearrange("p (k t) -> p k t", k=KC)
        halves = [h[:, :, :].bitcast(bf16).rearrange("p (n t) c -> p n t c", t=KC) for h in h1]
        parts = [[halves[1][:, 0], halves[1][:, 1], halves[1][:, 2]],
                 [halves[1][:, 3], halves[0][:, 2], halves[0][:, 3]]]
        k1_raw = h2[0][:, :, :].rearrange("p a t -> p (a t)").bitcast(u8)[:, 0:KF * F].rearrange("p (k f) -> p k f", k=KF)
        h2l_raw = h2[1][:, :, :].rearrange("p a t -> p (a t)").bitcast(u8)
        k0_raw = h2l_raw[:, 0:2 * KC * F].rearrange("p (k f) -> p k f", k=2 * KC)
        k2_raw = h2l_raw[:, 2 * KC * F:2 * KC * F + KF * C].rearrange("p (k c) -> p k c", k=KF)
        wq_raw = att[:, :, 0:C]
        wk_raw = sums[:, :, 0:C]

        psA = ctx.enter_context(nc.psum_tensor("psA", [P, 2, T], f32))
        psB = ctx.enter_context(nc.psum_tensor("psB", [P, 2, T], f32))
        psV = ctx.enter_context(nc.psum_tensor("psV", [P, T], f32))
        psC = ctx.enter_context(nc.psum_tensor("psC", [P, 3, T], f32))

        s_wts = sem("weights_loaded")
        s_scl = sem("scalars_loaded")
        s_zero = sem("pool_cleared")
        s_const = sem("constants_ready")
        s_wqk = sem("wqk_ready")
        s_sgn = sem("signs_ready")
        s_sgs = sem("signs_steps")
        s_w0d = sem("w0_difference")
        s_wffn = sem("ffn_weights_ready")
        s_x = sem("x_loaded")
        s_xT = sem("xT_in_psum")
        s_xnT = sem("xnT_ready")
        s_qk = sem("qk_in_psum")
        s_hi = sem("qk_high_ready")
        s_r1 = sem("qk_rest_ready")
        s_mid = sem("qk_mid_ready")
        s_lo = sem("qk_low_ready")
        s_stack = [sem(f"stacked_{w}") for w in "qk"]
        s_vps = sem("v_in_psum")
        s_v = sem("v_ready")
        s_s = sem("scores_in_psum")
        s_max = sem("max_taken")
        s_seen = sem("waits_apart")
        s_mstep = sem("max_part_steps")
        s_mparts = sem("max_parts_ready")
        s_mTps = sem("maxT_in_psum")
        s_mT = sem("maxT_ready")
        s_shift = sem("shift_rows_loaded")
        s_st = sem("scoresT_in_psum")
        s_exp = sem("exp_done")
        s_tri = sem("probs_masked")
        s_pv = sem("pv_done")
        s_o = sem("pv_copied")
        s_pack = [sem(f"packed{n}") for n in range(2)]
        s_rec = sem("sums_inverted")
        s_att = sem("attention_divided")
        s_res = sem("residual_loaded")
        s_xb = sem("residual_plus_beta")
        s_wo = sem("wo_in_psum")
        s_y = sem("y_ready")
        s_yg = sem("y_times_gamma")
        s_x1 = sem("x1_ready")
        s_c = sem("ffn_in_psum")
        s_ch = sem("ffn_high_ready")
        s_cl = sem("ffn_bank_read")
        s_out = sem("out_stored")

        class Norm:
            def __init__(self, tag):
                self.stats = sb(f"stats_{tag}", [P, NT, 6], f32)
                self.mv = sb(f"mv_{tag}", [P, NT, 2], f32)
                self.ve = sb(f"ve_{tag}", [P, NT], f32)
                self.rstd = sb(f"rstd_{tag}", [P, NT], f32)
                self.s_stats, self.s_mv, self.s_ve, self.s_rstd, self.s_out = (
                    sem(f"{tag}_{w}") for w in ("stats", "mean_var", "var_eps", "rstd", "normed"))

        ln1, lny, ln2 = Norm("ln1"), Norm("lny"), Norm("ln2")
        block = ctx.enter_context(nc.Block())

        def past(row, first=0):
            return not isinstance(row, int) or row > first

        def run(eng, iteration):
            for i in range(LOOP0):
                iteration(i, i % 2)
            with eng.Fori(LOOP0, LOOP1 - 1, 2) as i:
                iteration(i, LOOP0 % 2, True)
                iteration(i + 1, (LOOP0 + 1) % 2, True)
            for i in range(LOOP1, B + 3):
                iteration(i, i % 2)

        def stages(i, looped):
            def row(n):
                return n if looped or 0 <= n < B else None
            return row(i), row(i - 1), row(i - 2), row(i - 3), row(i + 1)

        SUB, FFN_START, S_START = 4, 5, 9
        STEPS = SUB * NS
        PIECES = KF * KC + KF * KF

        def spread(step, total, first, last):
            def upto(n):
                return min(total, max(0, -(-(n - first) * total // (last - first))))
            return range(upto(step), upto(step + 1))

        def s_units(step):
            return spread(step, NU, SUB * S_START, STEPS)

        def ffn_pieces(step):
            return spread(step, PIECES, SUB * FFN_START, STEPS - SUB)

        def ffn_done(step):
            ends = [KC * (m + 1) - 1 for m in range(KF)] + [KC * KF + KF * (m + 1) - 1 for m in range(KF)]
            return [2 + ends.index(n) for n in ffn_pieces(step) if n in ends]

        def c_bank(u):
            return psC[:, u % 3, :]

        @block.sync
        def _(sp):
            sp.dma_start(x_in[:, :, :], xv[0]).then_inc(s_x, 16)
            sp.dma_start(wq_raw, Wq.rearrange("(k p) n -> p k n", p=P)).then_inc(s_wts, 16)
            sp.dma_start(wk_raw, Wk.rearrange("(k p) n -> p k n", p=P)).then_inc(s_wts, 16)
            sp.dma_start(wv[:, :, :], Wv.rearrange("(k p) n -> p k n", p=P)).then_inc(s_wts, 16)
            with nc.allow_non_contiguous_dma(reason="biases to partitions in (d, head) order"):
                for j in range(4):
                    b = (bq, bk)[j // 2]
                    src = b[(j % 2) * P:(j % 2 + 1) * P].rearrange("(h d o) -> d h o", d=D, o=1)
                    sp.dma_start(bqk[:, j:j + 1], src).then_inc(s_wts, 16)
            for n, r in enumerate((bv, bo, gamma, beta)):
                sp.dma_start(rows[:, n, :], r.partition_broadcast(P)).then_inc(s_wts, 16)
            for n, s in enumerate((s0, s1, s2)):
                sp.dma_start(sc[:, n:n + 1], s.partition_broadcast(P)).then_inc(s_scl, 16)
            sp.dma_start(k0_raw, k0.rearrange("(k p) f -> p k f", p=P)).then_inc(s_scl, 16)
            sp.dma_start(k1_raw, k1.rearrange("(k p) f -> p k f", p=P)).then_inc(s_scl, 16)
            sp.dma_start(k2_raw, k2.rearrange("(k p) c -> p k c", p=P)).then_inc(s_scl, 16)
            sp.dma_start(wo[:, :, :], Wo.rearrange("(k p) n -> p k n", p=P)).then_inc(s_wts, 16)

            def stack(a, par, kind):
                dst, slots = (qS, kS)[kind][par], (SLOT_Q, SLOT_K)[kind]
                for part in range(3):
                    sp.wait_ge((s_hi, s_mid, s_lo)[part], 4 * a + 2 * kind + 2)
                    for n in range(len(slots)):
                        if slots[n] == part:
                            sp.dma_start(dst[16 * n:16 * n + 16, :, :],
                                         parts[kind][part]).then_inc(s_stack[kind], 16)

            def pack(b, g):
                sp.wait_ge(s_o, NG * b + g + 1)
                r = (g % 2) * 64
                sp.dma_start(asum[r:r + 64, :, g // 2, :], osum[g % 2][:, :]).then_inc(s_pack[g % 2], 16)

            def store(c, par, n):
                sp.wait_ge(s_cl, NC_USES * c + NC_USES - 1 + n)
                sp.dma_start(ov[c][:, 2 * n:2 * n + 2, :], x1[par][:, 2 * n:2 * n + 2, :]).then_inc(s_out, 16)

            def iteration(i, par, looped=False):
                a, b, c, cr, an = stages(i, looped)
                if a is not None:
                    stack(a, par, 0)
                if b is not None:
                    sp.wait_ge(s_mT, b + 1)
                    dst = qS[1 - par][ROWS_QK:ROWS_SHIFT, :, :].rearrange("r h (n e q) -> r e h n q", e=2, q=P)
                    for e in range(2):
                        sp.dma_start(dst[:, e], mT[3 * H * e:3 * H * (e + 1), :, :]).then_inc(s_shift, 16)
                if cr is not None:
                    store(cr, 1 - par, 1)
                if b is not None:
                    if past(b, 1):
                        sp.wait_ge(s_out, 32 * (b - 1))
                    sp.dma_start(x1[1 - par][:, :, :], xv[b]).then_inc(s_res, 16)
                if an is not None:
                    sp.wait_ge(s_xT, 2 * an)
                    sp.dma_start(x_in[:, :, :], xv[an]).then_inc(s_x, 16)
                if a is not None:
                    stack(a, par, 1)
                if b is not None:
                    for g in range(NG):
                        pack(b, g)
                if c is not None:
                    store(c, par, 0)

            run(sp, iteration)
            sp.wait_ge(s_out, 32 * B)

        @block.gpsimd
        def _(pool):
            pool.memset(ident[:, :], 0.0)
            pool.memset(identh[:, :], 0.0)
            pool.memset(causal[:, :], 0.0)
            pool.memset(neghalf[:, :], -0.5).then_inc(s_zero, 1)
            pool.wait_ge(s_zero, 1)
            for m in (ident, identh):
                pool.affine_select(out=m[:, :], in_=m[:, :], compare_op=ALU.not_equal, fill=1.0, base=0,
                                   pattern=[[-1, P]], channel_multiplier=1)
            diag = causal[:, T - P:T]
            pool.affine_select(out=diag, in_=diag, compare_op=ALU.is_ge, fill=-3.0e38, base=0,
                               pattern=[[-1, P]], channel_multiplier=1).then_inc(s_const, 1)

            def rstd(ln, row):
                pool.wait_ge(ln.s_ve, row + 1)
                pool.tensor_tensor(ln.rstd[:, :], ln.ve[:, :], neghalf[:, :], ALU.pow).then_inc(ln.s_rstd, 1)

            rstd(ln1, 0)
            pool.wait_ge(s_scl, 16 * 6)
            pool.wait_ge(s_sgn, 1)
            for k in range(KF):
                pool.tensor_scalar(w1[:, k, :], k1_raw[:, k, :], sc[:, 5:6], sc[:, 6:7], ALU.mult, ALU.add)
            pool.tensor_scalar(w2[:, :, :], k2_raw, 2.0, -1.0, ALU.mult, ALU.add).then_inc(s_wffn, 1)

            def triangle(b, s):
                j, pr = s // 2, s % 2
                pool.wait_ge(s_exp, NS * b + s + 1)
                pool.sem_inc(s_seen, 1)
                p = probs[j % 2][:, 2 * pr:2 * pr + 2, 0:P]
                pool.affine_select(out=p, in_=p, compare_op=ALU.is_ge, fill=0.0, base=0,
                                   pattern=[[0, 2], [1, P]], channel_multiplier=-1).then_inc(s_tri, 1)

            def iteration(i, par, looped=False):
                a, b, c, cr, an = stages(i, looped)
                if c is not None:
                    rstd(lny, c)
                    rstd(ln2, c)
                for s in range(NS):
                    if b is not None:
                        triangle(b, s)
                    if b is not None and s == 20:
                        pool.wait_ge(s_res, 16 * (b + 1))
                        pool.tensor_tensor(x1[1 - par][:, :, :], x1[1 - par][:, :, :],
                                           beta_r[:, None, :].to_broadcast([P, NT, C]), ALU.add).then_inc(s_xb, 1)
                    if s == 16 and an is not None:
                        rstd(ln1, an)

            run(pool, iteration)

        @block.scalar
        def _(act):
            act.wait_ge(s_wts, 16 * 12)

            def qk_high(a, j):
                act.wait_ge(s_qk, 4 * a + j + 1)
                if past(a):
                    act.wait_ge(s_stack[j // 2], 96 * a)
                act.activation(parts[j // 2][0][:, j % 2, :], psA[:, j % 2, :], ACT.Identity,
                               bias=bqk[:, j:j + 1]).then_inc(s_hi, 1)

            def ffn_high(c, u):
                act.wait_ge(s_c, NC_USES * c + u + 1)
                if u < 2:
                    act.activation(zT[0][:, u, :], c_bank(u), ACT.Copy).then_inc(s_ch, 1)
                else:
                    h = (h1 if u < 2 + KF else h2)[0]
                    act.activation(h[:, (u - 2) % KF, :], c_bank(u), ACT.Relu).then_inc(s_ch, 1)

            def exp(b, s):
                g, kb, pr = s // 8, (s % 8) // 2, s % 2
                j, n = s // 2, T - P * kb
                act.wait_ge(s_st, NS * b + s + 1)
                if past(b) or j > 1:
                    act.wait_ge(s_pv, (NS // 2) * b + j - 1)
                act.activation(probs[j % 2][:, 2 * pr:2 * pr + 2, 0:n], psB[:, :, 0:n], ACT.Exp,
                               scale=D ** -0.5).then_inc(s_exp, 1)

            def pv_copy(b, g):
                act.wait_ge(s_pv, (NS // 2) * b + 4 * g + 4)
                if past(b) or g > 1:
                    act.wait_ge(s_pack[g % 2], 16 * (2 * b + g // 2))
                act.activation(osum[g % 2][:, :], psV[:, :], ACT.Copy).then_inc(s_o, 1)

            def iteration(i, par, looped=False):
                a, b, c, cr, an = stages(i, looped)
                if a is not None:
                    for k in range(KC):
                        act.wait_ge(s_xT, 2 * a + k + 1)
                        act.activation(xnT[:, k, :], psA[:, k, :], ACT.Copy).then_inc(s_xnT, 1)
                    qk_high(a, 0)
                    qk_high(a, 1)
                if b is not None:
                    act.wait_ge(s_mTps, b + 1)
                    if past(b):
                        act.wait_ge(s_shift, 32 * b)
                    act.activation(mT[:, :, :].rearrange("r n q -> r (n q)"),
                                   psV[0:2 * 3 * H, :].bitcast(bf16)[:, 0:T // 2], ACT.Copy).then_inc(s_mT, 1)
                if a is not None:
                    qk_high(a, 2)
                    qk_high(a, 3)
                for step in range(STEPS):
                    s = step // SUB
                    if b is not None and step % SUB == 0:
                        exp(b, s)
                        if s % 8 == 2 and s > 8:
                            pv_copy(b, s // 8 - 1)
                    if c is not None:
                        if step == SUB * FFN_START - SUB:
                            ffn_high(c, 0)
                            ffn_high(c, 1)
                            if a is not None:
                                act.wait_ge(s_stack[0], 96 * (a + 1))
                                act.wait_ge(s_stack[1], 96 * (a + 1))
                        for u in ffn_done(step - 1):
                            ffn_high(c, u)
                if b is not None:
                    pv_copy(b, NG - 1)

            run(act, iteration)

        @block.vector
        def _(dve):
            def norm_stats(ln, row, src):
                for n in range(NT):
                    last = dve.bn_stats(ln.stats[:, n, :], src[:, n, :])
                last.then_inc(ln.s_stats, 1)
                dve.wait_ge(ln.s_stats, row + 1)
                dve.sem_inc(s_seen, 1)
                for n in range(NT):
                    last = dve.bn_aggr(ln.mv[:, n, :], ln.stats[:, n, :])
                last.then_inc(ln.s_mv, 1)
                dve.wait_ge(ln.s_mv, row + 1)
                dve.tensor_scalar(ln.ve[:, :], ln.mv[:, :, 1], EPS, None, ALU.add).then_inc(ln.s_ve, 1)

            def norm_apply(ln, row, dst, src):
                dve.wait_ge(ln.s_rstd, row + 1)
                for n in range(NT):
                    last = dve.tensor_scalar(dst[:, n, :], src[:, n, :], ln.mv[:, n, 0:1], ln.rstd[:, n:n + 1],
                                             ALU.subtract, ALU.mult)
                last.then_inc(ln.s_out, 1)

            dve.wait_ge(s_x, 16)
            dve.wait_ge(s_const, 1)
            norm_stats(ln1, 0, x_in)
            dve.wait_ge(s_wts, 16 * 12)
            for j in range(4):
                raw = (wq_raw, wk_raw)[j // 2]
                for k in range(KC):
                    last = dve.tensor_copy(
                        wqk[:, j, k, :].rearrange("p (d h) -> p d h", h=HT),
                        raw[:, k, (j % 2) * P:(j % 2 + 1) * P].rearrange("p (h d) -> p d h", d=D))
            last.then_inc(s_wqk, 1)
            norm_apply(ln1, 0, x_in, x_in)
            for n in range(2):
                dve.memset(vv[n][:, :, :, :, 1].rearrange("p n h d -> p (n h) d"), 1.0)
                dve.memset(kS[n][ROWS_QK:ROWS_SHIFT, :, :], 1.0)
            dve.wait_ge(s_scl, 16 * 6)
            steps = [0]

            def step(ins):
                steps[0] += 1
                ins.then_inc(s_sgs, 1)
                dve.wait_ge(s_sgs, steps[0])

            step(dve.tensor_scalar(sc[:, 8:10], sc[:, 0:2], 0.0, None, ALU.is_gt))
            step(dve.tensor_scalar(sc[:, 10:12], sc[:, 0:2], 0.0, None, ALU.is_lt))
            step(dve.tensor_tensor(sc[:, 12:14], sc[:, 8:10], sc[:, 10:12], ALU.subtract))
            step(dve.tensor_scalar(sc[:, 3:4], sc[:, 12:13], 2.0, None, ALU.mult))
            step(dve.tensor_scalar(sc[:, 5:6], sc[:, 13:14], 2.0 * H2_SCALE, None, ALU.mult))
            dve.tensor_scalar(sc[:, 6:7], sc[:, 13:14], -H2_SCALE, None, ALU.mult).then_inc(s_sgn, 1)
            step(dve.tensor_tensor(sc[:, 14:16], sc[:, 0:2], sc[:, 12:14], ALU.mult))
            step(dve.tensor_tensor(sc[:, 8:9], sc[:, 14:15], sc[:, 15:16], ALU.mult))
            step(dve.tensor_tensor(sc[:, 9:10], sc[:, 8:9], sc[:, 2:3], ALU.mult))
            step(dve.tensor_scalar(sc[:, 7:8], sc[:, 9:10], 4.0 / H2_SCALE, None, ALU.mult))
            for k in range(KC):
                last = dve.tensor_tensor(w0[:, k, :], k0_raw[:, k, :], k0_raw[:, KC + k, :], ALU.subtract)
            last.then_inc(s_w0d, 1)
            dve.wait_ge(s_w0d, 1)
            dve.tensor_scalar(w0[:, :, :], w0[:, :, :], sc[:, 3:4], None, ALU.mult).then_inc(s_wffn, 1)

            def qk_parts(a, j):
                high, mid, low = (part[:, j % 2, :] for part in parts[j // 2])
                if past(a) or j > 0:
                    dve.wait_ge(s_lo, 4 * a + j)
                if j == 0 and past(a):
                    dve.wait_ge(s_mparts, a)
                dve.wait_ge(s_hi, 4 * a + j + 1)
                dve.scalar_tensor_tensor(out=resid[:, :], in0=psA[:, j % 2, :], scalar=bqk[:, j:j + 1], in1=high,
                                         op0=ALU.add, op1=ALU.subtract).then_inc(s_r1, 1)
                dve.wait_ge(s_r1, 4 * a + j + 1)
                dve.tensor_copy(mid, resid[:, :]).then_inc(s_mid, 1)
                dve.wait_ge(s_mid, 4 * a + j + 1)
                dve.tensor_tensor(low, resid[:, :], mid, ALU.subtract).then_inc(s_lo, 1)

            def v_copy(a, par, n):
                dve.wait_ge(s_vps, 2 * a + n + 1)
                for e in range(2):
                    last = dve.tensor_tensor(
                        vv[par][:, 2 * n + e, :, :, 0],
                        psA[:, n, e * C:(e + 1) * C].rearrange("p (h d) -> p h d", d=D),
                        bv_r.rearrange("p (h d) -> p h d", d=D), ALU.add)
                last.then_inc(s_v, 1)

            def unit_max(a, u):
                h, qb = u // NT, u % NT
                n = (qb + 1) * P
                dve.wait_ge(s_s, NU * a + u + 1)
                dve.sem_inc(s_seen, 1)
                sc_ = psA[:, u % 2, 0:n]
                dve.tensor_tensor_reduce(out=sc_, in0=sc_, in1=causal[:, T - n:T], scale=1.0, scalar=-3.0e38,
                                         op0=ALU.add, op1=ALU.max, accum_out=rowmax[:, qb, h:h + 1]).then_inc(s_max, 1)

            def max_parts(a):
                dve.wait_ge(s_max, NU * (a + 1))
                if past(a):
                    dve.wait_ge(s_mTps, a)
                part = [mparts[:, :, H * n:H * n + H] for n in range(3)]
                dve.tensor_scalar(part[0], rowmax[:, :, :], -1.0, None, ALU.mult).then_inc(s_mstep, 1)
                dve.wait_ge(s_mstep, 3 * a + 1)
                dve.scalar_tensor_tensor(out=negr[:, :, :], in0=rowmax[:, :, :], scalar=-1.0, in1=part[0],
                                         op0=ALU.mult, op1=ALU.subtract).then_inc(s_mstep, 1)
                dve.wait_ge(s_mstep, 3 * a + 2)
                dve.tensor_copy(part[1], negr[:, :, :]).then_inc(s_mstep, 1)
                dve.wait_ge(s_mstep, 3 * a + 3)
                dve.tensor_tensor(part[2], negr[:, :, :], part[1], ALU.subtract).then_inc(s_mparts, 1)

            def divide(b, t):
                dve.wait_ge(s_pack[0], 16 * (2 * b + t + 1))
                dve.wait_ge(s_pack[1], 16 * (2 * b + t + 1))
                dve.reciprocal(sums[:, t, :], sums[:, t, :]).then_inc(s_rec, 1)
                dve.wait_ge(s_rec, KC * b + t + 1)
                dve.tensor_tensor(att[:, t, :], att[:, t, :], sums[:, t, :], ALU.mult).then_inc(s_att, 1)

            def ffn_low(c, u):
                dve.wait_ge(s_ch, (NC_USES - 2) * c + u + 1)
                if u < 2:
                    dve.tensor_tensor(zT[1][:, u, :], c_bank(u), zT[0][:, u, :], ALU.subtract).then_inc(s_cl, 1)
                else:
                    h, m = (h1 if u < 2 + KF else h2), (u - 2) % KF
                    dve.scalar_tensor_tensor(out=h[1][:, m, :], in0=c_bank(u), scalar=0.0, in1=h[0][:, m, :],
                                             op0=ALU.max, op1=ALU.subtract).then_inc(s_cl, 1)

            def finish(c, par, n):
                u = NC_USES - 2 + n
                dve.wait_ge(s_c, NC_USES * c + u + 1)
                o = x1[par][:, 2 * n:2 * n + 2, :].rearrange("p n c -> p (n c)")
                dve.scalar_tensor_tensor(out=o, in0=c_bank(u), scalar=sc[:, 7:8], in1=o,
                                         op0=ALU.mult, op1=ALU.add).then_inc(s_cl, 1)

            def iteration(i, par, looped=False):
                a, b, c, cr, an = stages(i, looped)
                if a is not None:
                    qk_parts(a, 0)
                    qk_parts(a, 1)
                if c is not None:
                    for n in range(2):
                        dve.wait_ge(s_wo, 2 * c + n + 1)
                        dve.tensor_tensor(y[:, 2 * n:2 * n + 2, :],
                                          psB[:, n, :].rearrange("p (n c) -> p n c", n=2),
                                          bo_r[:, None, :].to_broadcast([P, 2, C]), ALU.add).then_inc(s_y, 1)
                    dve.wait_ge(s_y, 2 * c + 2)
                    norm_stats(lny, c, y)
                if a is not None:
                    for n in range(2):
                        v_copy(a, par, n)
                if c is not None:
                    dve.wait_ge(lny.s_rstd, c + 1)
                    for n in range(NT):
                        last = dve.scalar_tensor_tensor(out=y[:, n, :], in0=y[:, n, :], scalar=lny.mv[:, n, 0:1],
                                                        in1=gamma_r, op0=ALU.subtract, op1=ALU.mult)
                    last.then_inc(s_yg, 1)
                    dve.wait_ge(s_yg, c + 1)
                    dve.wait_ge(s_xb, c + 1)
                    xr = x1[par]
                    for n in range(NT):
                        last = dve.scalar_tensor_tensor(out=xr[:, n, :], in0=y[:, n, :], scalar=lny.rstd[:, n:n + 1],
                                                        in1=xr[:, n, :], op0=ALU.mult, op1=ALU.add)
                    last.then_inc(s_x1, 1)
                    dve.wait_ge(s_x1, c + 1)
                    norm_stats(ln2, c, xr)
                if cr is not None:
                    finish(cr, 1 - par, 1)
                if c is not None:
                    norm_apply(ln2, c, y, x1[par])
                if a is not None:
                    qk_parts(a, 2)
                if c is not None:
                    ffn_low(c, 0)
                    ffn_low(c, 1)
                if a is not None:
                    qk_parts(a, 3)
                for step in range(STEPS):
                    s = step // SUB
                    if a is not None:
                        for u in s_units(step):
                            unit_max(a, u)
                    if c is not None:
                        for u in ffn_done(step - 2):
                            ffn_low(c, u)
                    if an is not None and step == SUB * 14:
                        dve.wait_ge(s_x, 16 * (an + 1))
                        norm_stats(ln1, an, x_in)
                    if an is not None and step == SUB * 18:
                        norm_apply(ln1, an, x_in, x_in)
                    if b is not None and step == SUB * 25:
                        divide(b, 0)
                if a is not None:
                    max_parts(a)
                if b is not None:
                    divide(b, 1)
                if c is not None:
                    finish(c, par, 0)

            run(dve, iteration)

        @block.tensor
        def _(pe):
            pe.wait_ge(s_const, 1)
            pe.wait_ge(s_wqk, 1)
            pe.wait_ge(s_wts, 16 * 12)

            def x_transposed(a):
                pe.wait_ge(ln1.s_out, a + 1)
                if past(a):
                    pe.wait_ge(s_max, NU * a)
                for k in range(KC):
                    for n in range(NT):
                        last = pe.transpose(psA[:, k, n * P:(n + 1) * P], x_in[:, n, k * P:(k + 1) * P], ident[:, :])
                    last.then_inc(s_xT, 1)

            def qk(a, j):
                if j == 0:
                    pe.wait_ge(s_xnT, 2 * a + 2)
                if j >= 2:
                    pe.wait_ge(s_v, 2 * a + j - 1)
                for k in range(KC):
                    last = pe.matmul(psA[:, j % 2, :], wqk[:, j, k, :], xnT[:, k, :], start=(k == 0), stop=(k == KC - 1))
                last.then_inc(s_qk, 1)

            def v(a, n):
                pe.wait_ge(s_r1, 4 * a + 1 + n)
                for e in range(2):
                    t = 2 * n + e
                    for k in range(KC):
                        last = pe.matmul(psA[:, n, e * C:(e + 1) * C], xnT[:, k, t * P:(t + 1) * P], wv[:, k, :],
                                         start=(k == 0), stop=(k == KC - 1))
                last.then_inc(s_vps, 1)

            def scores(a, par, u):
                h, qb = u // NT, u % NT
                if u == 0:
                    pe.wait_ge(s_stack[0], 96 * (a + 1))
                    pe.wait_ge(s_stack[1], 96 * (a + 1))
                    pe.wait_ge(s_r1, 4 * a + 4)
                if u >= 2:
                    pe.wait_ge(s_max, NU * a + u - 1)
                n = (qb + 1) * P
                pe.matmul(psA[:, u % 2, 0:n], qS[par][0:ROWS_QK, h, qb * P:(qb + 1) * P],
                          kS[par][0:ROWS_QK, h, 0:n], start=True, stop=True).then_inc(s_s, 1)

            def max_transposed(b):
                pe.wait_ge(s_mparts, b + 1)
                if past(b):
                    pe.wait_ge(s_o, NG * b)
                o = psV[0:2 * 3 * H, :].bitcast(bf16)
                for n in range(NT // 2):
                    last = pe.transpose(o[:, n * P:(n + 1) * P],
                                        mparts[:, 2 * n:2 * n + 2, :].rearrange("q e m -> q (e m)"), identh[:, :])
                last.then_inc(s_mTps, 1)

            def scores_t(b, par, s):
                g, kb, pr = s // 8, (s % 8) // 2, s % 2
                if s == 0:
                    pe.wait_ge(s_shift, 32 * (b + 1))
                if past(b) or s > 0:
                    pe.wait_ge(s_exp, NS * b + s)
                if s == 0 and past(b):
                    pe.wait_ge(s_y, 2 * b)
                for e in range(2):
                    h = 4 * g + 2 * pr + e
                    last = pe.matmul(psB[:, e, 0:T - kb * P], kS[par][0:ROWS_SHIFT, place(h), kb * P:(kb + 1) * P],
                                     qS[par][0:ROWS_SHIFT, place(h), kb * P:T], start=True, stop=True)
                last.then_inc(s_st, 1)

            def pv(b, par, j):
                g, kb = j // NT, j % NT
                pe.wait_ge(s_tri, NS * b + 2 * j + 2)
                if kb == 0:
                    if g > 0:
                        pe.wait_ge(s_o, NG * b + g)
                    else:
                        pe.wait_ge(s_mT, b + 1)
                for i4 in range(4):
                    last = pe.matmul(psV[32 * i4:32 * i4 + 32, kb * P:T], vv[par][:, kb, 4 * g + i4].rearrange("p d e -> p (d e)"),
                                     probs[j % 2][:, i4, 0:T - kb * P], start=(kb == 0), stop=(kb == NT - 1))
                last.then_inc(s_pv, 1)

            def project(c):
                pe.wait_ge(s_att, KC * (c + 1))
                pe.wait_ge(s_exp, NS * (c + 1))
                for n in range(NT):
                    for t in range(KC):
                        last = pe.matmul(psB[:, n // 2, (n % 2) * C:(n % 2 + 1) * C], att[:, t, n * P:(n + 1) * P],
                                         wo[:, t, :], start=(t == 0), stop=(t == KC - 1))
                    if n % 2:
                        last.then_inc(s_wo, 1)

            def c_free(c, u):
                if past(c) or u > 2:
                    pe.wait_ge(s_cl, NC_USES * c + u - 2)

            def z_transposed(c):
                pe.wait_ge(ln2.s_out, c + 1)
                for u in range(KC):
                    c_free(c, u)
                    for n in range(NT):
                        last = pe.transpose(c_bank(u)[:, n * P:(n + 1) * P], y[:, n, u * P:(u + 1) * P], ident[:, :])
                    last.then_inc(s_c, 1)

            def ffn_piece(c, piece):
                first = piece < KC * KF
                m, k = divmod(piece, KC) if first else divmod(piece - KC * KF, KF)
                w, act_in, k_last, u = (w0, zT, KC - 1, 2 + m) if first else (w1, h1, KF - 1, 2 + KF + m)
                if k == 0:
                    c_free(c, u)
                if piece == 0:
                    pe.wait_ge(s_cl, NC_USES * c + 2)
                if not first and m == 0:
                    pe.wait_ge(s_cl, NC_USES * c + 2 + k + 1)
                for part in range(2):
                    last = pe.matmul(c_bank(u), w[:, k, m * P:(m + 1) * P], act_in[part][:, k, :],
                                     start=(k == 0 and part == 0), stop=(k == k_last and part == 1))
                if k == k_last:
                    last.then_inc(s_c, 1)

            def ffn3(c, n):
                u = NC_USES - 2 + n
                c_free(c, u)
                pe.wait_ge(s_cl, NC_USES * c + 2 + 2 * KF)
                for e in range(2):
                    t = 2 * n + e
                    for q, (k, part) in enumerate((k, part) for k in range(KF) for part in range(2)):
                        last = pe.matmul(c_bank(u)[:, e * C:(e + 1) * C], h2[part][:, k, t * P:(t + 1) * P], w2[:, k, :],
                                         start=(q == 0), stop=(q == 2 * KF - 1))
                last.then_inc(s_c, 1)

            def iteration(i, par, looped=False):
                a, b, c, cr, an = stages(i, looped)
                if a is not None:
                    x_transposed(a)
                    qk(a, 0)
                    qk(a, 1)
                if c is not None:
                    project(c)
                if b is not None:
                    max_transposed(b)
                if a is not None:
                    v(a, 0)
                    v(a, 1)
                    qk(a, 2)
                    qk(a, 3)
                if cr is not None:
                    ffn3(cr, 1)
                for step in range(STEPS):
                    s = step // SUB
                    if b is not None and step % SUB == 0:
                        scores_t(b, 1 - par, s)
                    if b is not None and step % (2 * SUB) == SUB + 2 and s >= 3:
                        pv(b, 1 - par, (s - 3) // 2)
                    if c is not None and step == SUB * FFN_START - SUB + 1:
                        if not looped and c == 0:
                            pe.wait_ge(s_wffn, 2)
                        z_transposed(c)
                    if a is not None:
                        for u in s_units(step):
                            scores(a, par, u)
                    if c is not None:
                        for piece in ffn_pieces(step):
                            ffn_piece(c, piece)
                if b is not None:
                    pv(b, 1 - par, NS // 2 - 1)
                if c is not None:
                    ffn3(c, 0)

            run(pe, iteration)


_INS = ["L0_attn_x", "L0_attn_Wq", "L0_attn_bq", "L0_attn_Wk", "L0_attn_bk", "L0_attn_Wv", "L0_attn_bv",
        "L0_attn_Wo", "L0_attn_bo", "L0_attn_gamma", "L0_attn_beta", "L0_ffn_k0", "L0_ffn_k1", "L0_ffn_k2",
        "L0_ffn_s0", "L0_ffn_s1", "L0_ffn_s2"]


def kernel(**inputs):
    import numpy as np
    import concourse.bacc as bacc
    from concourse.bass_utils import run_bass_kernel_spmd

    nc = bacc.Bacc("TRN2", target_bir_lowering=False, num_devices=1)
    arrays, args = {}, []
    for name in _INS:
        a = np.ascontiguousarray(inputs[name])
        a = a.reshape(a.shape or (1,))
        arrays[f"in_{name}"] = a
        args.append(nc.dram_tensor(f"in_{name}", a.shape, mybir.dt.from_np(a.dtype), kind="ExternalInput").ap())
    shape = tuple(inputs["L0_attn_x"].shape)
    args.append(nc.dram_tensor("out_0", shape, mybir.dt.float32, kind="ExternalOutput").ap())
    layer_kernel(nc, *args)
    r = run_bass_kernel_spmd(nc, [arrays], core_ids=[0])
    return r.results[0]["out_0"]
```

```python
import concourse.bass as bass
from concourse import mybir
from contextlib import ExitStack

P = 128


def layer_kernel(nc, x, Wq, bq, Wk, bk, Wv, bv, Wo, bo, gamma, beta, k0, k1, k2, s0, s1, s2, out):
    f32, bf16, f16, u8 = mybir.dt.float32, mybir.dt.bfloat16, mybir.dt.float16, mybir.dt.uint8
    ALU, ACT, AX = mybir.AluOpType, mybir.ActivationFunctionType, mybir.AxisListType

    B, T, C = x.shape
    H = 16
    D = C // H
    F = k1.shape[0]
    EPS = 1e-5
    NT = T // P
    KC = C // P
    KF = F // P
    HT = H // KC
    SLOT_Q = (0, 0, 1, 1, 0, 2)
    SLOT_K = (0, 1, 0, 1, 2, 0)
    ROWS_QK = 16 * len(SLOT_Q)
    ROWS_SHIFT = ROWS_QK + 3
    QB = ((3,), (2, 0), (1,))
    NU = H * len(QB)
    NS = (H // 2) * NT
    NG = H // 4
    NC_USES = 2 + 2 * KF + 2
    H2_SCALE = 1.0 / 16.0
    LOOP0, LOOP1 = 3, 15

    xv = x.rearrange("b (n p) c -> b p n c", p=P)
    ov = out.rearrange("b (n p) c -> b p n c", p=P)

    ctx = ExitStack()
    with ctx:
        def place(h):
            return (h % HT) * KC + h // HT

        def sb(name, shape, dt):
            return ctx.enter_context(nc.sbuf_tensor(name, shape, dt))

        def sem(name):
            return ctx.enter_context(nc.semaphore(name))

        ident = sb("ident", [P, P], f32)
        identh = sb("identh", [P, P], bf16)
        causal = sb("causal", [P, T], bf16)
        wqk = sb("wqk", [P, 4, KC, P], f32)
        wv = sb("wv", [P, KC, C], f32)
        wo = sb("wo", [P, KC, C], f32)
        bqk = sb("bqk", [P, 4], f32)
        rows = sb("rows", [P, 4, C], f32)
        bv_r, bo_r, gamma_r, beta_r = (rows[:, n, :] for n in range(4))
        w0 = sb("w0", [P, KC, F], f16)
        w1 = sb("w1", [P, KF, F], f16)
        w2 = sb("w2", [P, KF, C], f16)
        sc = sb("sc", [P, 16], f32)
        neghalf = sb("neghalf", [P, NT], f32)
        x_in = sb("x_in", [P, NT, C], f32)
        resid = [sb(f"resid{n}", [P, T], f32) for n in range(2)]
        qS = [sb(f"qS{n}", [P, H, T], bf16) for n in range(2)]
        kS = [sb(f"kS{n}", [P, H, T], bf16) for n in range(2)]
        vv = [sb(f"vv{n}", [P, NT, H, D, 2], f32) for n in range(2)]
        rowmax = sb("rowmax", [P, NT, H], f32)
        negr = sb("negr", [P, NT, H], f32)
        mparts = sb("mparts", [P, NT, 3 * H], bf16)
        mT = sb("mT", [2 * 3 * H, NT // 2, P], bf16)
        probs = [sb(f"probs{n}", [P, 4, T], f32) for n in range(2)]
        osum = [sb(f"osum{n}", [P, T], f32) for n in range(2)]
        asum = sb("asum", [P, 2, KC, T], f32)
        att, sums = asum[:, 0], asum[:, 1]
        y = sb("y", [P, NT, C], f32)
        x1 = [sb(f"x1_{n}", [P, NT, C], f32) for n in range(2)]
        zT = [sb(f"zT{n}", [P, KC, T], f16) for n in ("h", "l")]
        h1 = [sb(f"h1{n}", [P, KF, T], f16) for n in ("h", "l")]
        h2 = [sb(f"h2{n}", [P, KF, T], f16) for n in ("h", "l")]
        xnT = h1[0][:, 0:2 * KC, :].rearrange("p a t -> p (a t)").bitcast(f32).rearrange("p (k t) -> p k t", k=KC)
        halves = [h[:, :, :].bitcast(bf16).rearrange("p (n t) c -> p n t c", t=KC) for h in h1]
        parts = [[halves[1][:, 0], halves[1][:, 1], halves[1][:, 2]],
                 [halves[1][:, 3], halves[0][:, 2], halves[0][:, 3]]]
        k1_raw = h2[0][:, :, :].rearrange("p a t -> p (a t)").bitcast(u8)[:, 0:KF * F].rearrange("p (k f) -> p k f", k=KF)
        h2l_raw = h2[1][:, :, :].rearrange("p a t -> p (a t)").bitcast(u8)
        k0_raw = h2l_raw[:, 0:2 * KC * F].rearrange("p (k f) -> p k f", k=2 * KC)
        k2_raw = h2l_raw[:, 2 * KC * F:2 * KC * F + KF * C].rearrange("p (k c) -> p k c", k=KF)
        wq_raw = att[:, :, 0:C]
        wk_raw = sums[:, :, 0:C]

        psA = ctx.enter_context(nc.psum_tensor("psA", [P, 2, T], f32))
        psB = ctx.enter_context(nc.psum_tensor("psB", [P, 2, T], f32))
        psV = ctx.enter_context(nc.psum_tensor("psV", [P, T], f32))
        psC = ctx.enter_context(nc.psum_tensor("psC", [P, 3, T], f32))

        s_wraw = sem("wq_wk_loaded")
        s_wts = sem("weights_loaded")
        s_kraw = sem("ffn_bits_loaded")
        s_ones = sem("ones_under_k")
        s_scl = sem("scalars_loaded")
        s_zero = sem("pool_cleared")
        s_const = sem("constants_ready")
        s_wqk = sem("wqk_ready")
        s_sgn = sem("signs_ready")
        s_sgs = sem("signs_steps")
        s_w0d = sem("w0_difference")
        s_wffn = sem("ffn_weights_ready")
        s_x = sem("x_loaded")
        s_xT = sem("xT_in_psum")
        s_xnT = sem("xnT_ready")
        s_qk = sem("qk_in_psum")
        s_hi = sem("qk_high_ready")
        s_r1 = sem("qk_rest_ready")
        s_mid = sem("qk_mid_ready")
        s_lo = sem("qk_low_ready")
        s_stack = [sem(f"stacked_{w}") for w in "qk"]
        s_vps = sem("v_in_psum")
        s_v = sem("v_ready")
        s_s = sem("scores_in_psum")
        s_max = sem("max_taken")
        s_seen = sem("waits_apart")
        s_mstep = sem("max_part_steps")
        s_mparts = sem("max_parts_ready")
        s_mTps = sem("maxT_in_psum")
        s_mT = sem("maxT_ready")
        s_shift = sem("shift_rows_loaded")
        s_st = sem("scoresT_in_psum")
        s_exp = sem("exp_done")
        s_tri = sem("probs_masked")
        s_pv = sem("pv_done")
        s_o = sem("pv_copied")
        s_pack = [sem(f"packed{n}") for n in range(2)]
        s_rec = sem("sums_inverted")
        s_att = sem("attention_divided")
        s_res = sem("residual_loaded")
        s_xb = sem("residual_plus_beta")
        s_wo = sem("wo_in_psum")
        s_y = sem("y_ready")
        s_yg = sem("y_times_gamma")
        s_x1 = sem("x1_ready")
        s_c = sem("ffn_in_psum")
        s_ch = sem("ffn_high_ready")
        s_cl = sem("ffn_bank_read")
        s_out = sem("out_stored")

        class Norm:
            def __init__(self, tag):
                self.stats = sb(f"stats_{tag}", [P, NT, 6], f32)
                self.mv = sb(f"mv_{tag}", [P, NT, 2], f32)
                self.ve = sb(f"ve_{tag}", [P, NT], f32)
                self.rstd = sb(f"rstd_{tag}", [P, NT], f32)
                self.s_stats, self.s_mv, self.s_ve, self.s_rstd, self.s_out = (
                    sem(f"{tag}_{w}") for w in ("stats", "mean_var", "var_eps", "rstd", "normed"))

        ln1, lny, ln2 = Norm("ln1"), Norm("lny"), Norm("ln2")
        block = ctx.enter_context(nc.Block())

        def past(row, first=0):
            return not isinstance(row, int) or row > first

        def run(eng, iteration):
            for i in range(LOOP0):
                iteration(i, i % 2)
            with eng.Fori(LOOP0, LOOP1 - 1, 2) as i:
                iteration(i, LOOP0 % 2, True)
                iteration(i + 1, (LOOP0 + 1) % 2, True)
            for i in range(LOOP1, B + 3):
                iteration(i, i % 2)

        def stages(i, looped):
            def row(n):
                return n if looped or 0 <= n < B else None
            return row(i), row(i - 1), row(i - 2), row(i - 3), row(i + 1)

        SUB, FFN_START, S_START = 4, 5, 6
        STEPS = SUB * NS
        PIECES = KF * KC + KF * KF

        def spread(step, total, first, last):
            def upto(n):
                return min(total, max(0, -(-(n - first) * total // (last - first))))
            return range(upto(step), upto(step + 1))

        def s_units(step):
            return spread(step, NU, SUB * S_START, STEPS)

        def ffn_pieces(step):
            return spread(step, PIECES, SUB * FFN_START, STEPS - 2)

        def ffn_done(step):
            ends = [KC * (m + 1) - 1 for m in range(KF)] + [KC * KF + KF * (m + 1) - 1 for m in range(KF)]
            return [2 + ends.index(n) for n in ffn_pieces(step) if n in ends]

        def s_banks(c):
            own = [psA[:, n, :] for n in range(2)]
            return own if c is not None else own + [psC[:, n, :] for n in range(3)]

        def c_bank(u):
            return psC[:, 2 if u == NC_USES - 1 else u % 3, :]

        @block.sync
        def _(sp):
            sp.dma_start(x_in[:, :, :], xv[0]).then_inc(s_x, 16)
            sp.dma_start(wq_raw, Wq.rearrange("(k p) n -> p k n", p=P)).then_inc(s_wraw, 16)
            sp.dma_start(wk_raw, Wk.rearrange("(k p) n -> p k n", p=P)).then_inc(s_wraw, 16)
            for n, s in enumerate((s0, s1, s2)):
                sp.dma_start(sc[:, n:n + 1], s.partition_broadcast(P)).then_inc(s_scl, 16)
            with nc.allow_non_contiguous_dma(reason="biases to partitions in (d, head) order"):
                for j in range(4):
                    b = (bq, bk)[j // 2]
                    src = b[(j % 2) * P:(j % 2 + 1) * P].rearrange("(h d o) -> d h o", d=D, o=1)
                    sp.dma_start(bqk[:, j:j + 1], src).then_inc(s_wts, 16)
            sp.dma_start(wv[:, :, :], Wv.rearrange("(k p) n -> p k n", p=P)).then_inc(s_wts, 16)
            for n, r in enumerate((bv, bo, gamma, beta)):
                sp.dma_start(rows[:, n, :], r.partition_broadcast(P)).then_inc(s_wts, 16)
            sp.dma_start(wo[:, :, :], Wo.rearrange("(k p) n -> p k n", p=P)).then_inc(s_wts, 16)
            sp.dma_start(k0_raw, k0.rearrange("(k p) f -> p k f", p=P)).then_inc(s_kraw, 16)
            sp.dma_start(k1_raw, k1.rearrange("(k p) f -> p k f", p=P)).then_inc(s_kraw, 16)
            sp.dma_start(k2_raw, k2.rearrange("(k p) c -> p k c", p=P)).then_inc(s_kraw, 16)

            def stack(a, par, kind):
                dst, slots = (qS, kS)[kind][par], (SLOT_Q, SLOT_K)[kind]
                for part in range(3):
                    sp.wait_ge((s_hi, s_mid, s_lo)[part], 4 * a + 2 * kind + 2)
                    for n in range(len(slots)):
                        if slots[n] == part:
                            sp.dma_start(dst[16 * n:16 * n + 16, :, :],
                                         parts[kind][part]).then_inc(s_stack[kind], 16)

            def pack(b, g):
                sp.wait_ge(s_o, NG * b + g + 1)
                r = (g % 2) * 64
                sp.dma_start(asum[r:r + 64, :, g // 2, :], osum[g % 2][:, :]).then_inc(s_pack[g % 2], 16)

            def store(c, par, n):
                sp.wait_ge(s_cl, NC_USES * c + NC_USES - 1 + n)
                sp.dma_start(ov[c][:, 2 * n:2 * n + 2, :], x1[par][:, 2 * n:2 * n + 2, :]).then_inc(s_out, 16)

            def iteration(i, par, looped=False):
                a, b, c, cr, an = stages(i, looped)
                if b is not None:
                    sp.wait_ge(s_mT, b + 1)
                    dst = qS[1 - par][ROWS_QK:ROWS_SHIFT, :, :].rearrange("r h (n e q) -> r e h n q", e=2, q=P)
                    for e in range(2):
                        sp.dma_start(dst[:, e], mT[3 * H * e:3 * H * (e + 1), :, :]).then_inc(s_shift, 16)
                if a is not None:
                    stack(a, par, 0)
                    stack(a, par, 1)
                if cr is not None:
                    store(cr, 1 - par, 0)
                    store(cr, 1 - par, 1)
                if b is not None:
                    if past(b, 1):
                        sp.wait_ge(s_out, 32 * (b - 1))
                    sp.dma_start(x1[1 - par][:, :, :], xv[b]).then_inc(s_res, 16)
                if an is not None:
                    sp.wait_ge(s_xT, 2 * an)
                    sp.dma_start(x_in[:, :, :], xv[an]).then_inc(s_x, 16)
                if b is not None:
                    for g in range(NG):
                        pack(b, g)
            run(sp, iteration)
            sp.wait_ge(s_out, 32 * B)

        @block.gpsimd
        def _(pool):
            pool.memset(ident[:, :], 0.0)
            pool.memset(identh[:, :], 0.0)
            pool.memset(causal[:, :], 0.0)
            pool.memset(neghalf[:, :], -0.5).then_inc(s_zero, 1)
            pool.wait_ge(s_zero, 1)
            for m in (ident, identh):
                pool.affine_select(out=m[:, :], in_=m[:, :], compare_op=ALU.not_equal, fill=1.0, base=0,
                                   pattern=[[-1, P]], channel_multiplier=1)
            diag = causal[:, T - P:T]
            pool.affine_select(out=diag, in_=diag, compare_op=ALU.is_ge, fill=-3.0e38, base=0,
                               pattern=[[-1, P]], channel_multiplier=1).then_inc(s_const, 1)

            def rstd(ln, row):
                pool.wait_ge(ln.s_ve, row + 1)
                pool.tensor_tensor(ln.rstd[:, :], ln.ve[:, :], neghalf[:, :], ALU.pow).then_inc(ln.s_rstd, 1)

            rstd(ln1, 0)
            pool.wait_ge(ln1.s_rstd, 1)
            for n in range(2):
                pool.memset(kS[n][ROWS_QK:ROWS_SHIFT, :, :], 1.0).then_inc(s_ones, 1)
                pool.wait_ge(s_ones, n + 1)

            def ffn_weights():
                pool.wait_ge(s_kraw, 16 * 3)
                pool.wait_ge(s_sgn, 1)
                for k in range(KF):
                    pool.tensor_scalar(w1[:, k, :], k1_raw[:, k, :], sc[:, 5:6], sc[:, 6:7], ALU.mult, ALU.add)
                pool.tensor_scalar(w2[:, :, :], k2_raw, 2.0, -1.0, ALU.mult, ALU.add).then_inc(s_wffn, 1)

            def qk_low(a, j):
                mid, low = (part[:, j % 2, :] for part in parts[j // 2][1:3])
                pool.wait_ge(s_mid, 4 * a + j + 1)
                pool.tensor_tensor(low, resid[j % 2][:, :], mid, ALU.subtract).then_inc(s_lo, 1)

            def triangle(b, s):
                j, pr = s // 2, s % 2
                pool.wait_ge(s_exp, NS * b + s + 1)
                pool.sem_inc(s_seen, 1)
                p = probs[j % 2][:, 2 * pr:2 * pr + 2, 0:P]
                pool.affine_select(out=p, in_=p, compare_op=ALU.is_ge, fill=0.0, base=0,
                                   pattern=[[0, 2], [1, P]], channel_multiplier=-1).then_inc(s_tri, 1)

            def iteration(i, par, looped=False):
                a, b, c, cr, an = stages(i, looped)
                if a is not None:
                    qk_low(a, 0)
                if c is not None:
                    rstd(lny, c)
                if a is not None:
                    qk_low(a, 1)
                for s in range(NS):
                    if s == 2 and c is not None:
                        rstd(ln2, c)
                    if s == 2 and a is not None:
                        qk_low(a, 2)
                    if s == 4 and a is not None:
                        qk_low(a, 3)
                    if s == 4 and not looped and i == 0:
                        ffn_weights()
                    if b is not None:
                        triangle(b, s)
                    if b is not None and s == 20:
                        pool.wait_ge(s_res, 16 * (b + 1))
                        pool.tensor_tensor(x1[1 - par][:, :, :], x1[1 - par][:, :, :],
                                           beta_r[:, None, :].to_broadcast([P, NT, C]), ALU.add).then_inc(s_xb, 1)
                    if s == 16 and an is not None:
                        rstd(ln1, an)

            run(pool, iteration)

        @block.scalar
        def _(act):
            act.wait_ge(s_wts, 16 * 10)

            def qk_high(a, j):
                act.wait_ge(s_qk, 4 * a + j + 1)
                if past(a):
                    act.wait_ge(s_stack[j // 2], 96 * a)
                act.activation(parts[j // 2][0][:, j % 2, :], psA[:, j % 2, :], ACT.Identity,
                               bias=bqk[:, j:j + 1]).then_inc(s_hi, 1)

            def ffn_high(c, u):
                act.wait_ge(s_c, NC_USES * c + u + 1)
                if u < 2:
                    act.activation(zT[0][:, u, :], c_bank(u), ACT.Copy).then_inc(s_ch, 1)
                else:
                    h = (h1 if u < 2 + KF else h2)[0]
                    act.activation(h[:, (u - 2) % KF, :], c_bank(u), ACT.Relu).then_inc(s_ch, 1)

            def exp(b, s):
                g, kb, pr = s // 8, (s % 8) // 2, s % 2
                j, n = s // 2, T - P * kb
                act.wait_ge(s_st, NS * b + s + 1)
                if past(b) or j > 1:
                    act.wait_ge(s_pv, (NS // 2) * b + j - 1)
                act.activation(probs[j % 2][:, 2 * pr:2 * pr + 2, 0:n], psB[:, :, 0:n], ACT.Exp,
                               scale=D ** -0.5).then_inc(s_exp, 1)

            def pv_copy(b, g):
                act.wait_ge(s_pv, (NS // 2) * b + 4 * g + 4)
                if past(b) or g > 1:
                    act.wait_ge(s_pack[g % 2], 16 * (2 * b + g // 2))
                act.activation(osum[g % 2][:, :], psV[:, :], ACT.Copy).then_inc(s_o, 1)

            def iteration(i, par, looped=False):
                a, b, c, cr, an = stages(i, looped)
                if a is not None:
                    for k in range(KC):
                        act.wait_ge(s_xT, 2 * a + k + 1)
                        act.activation(xnT[:, k, :], psA[:, k, :], ACT.Copy).then_inc(s_xnT, 1)
                    qk_high(a, 0)
                if b is not None:
                    act.wait_ge(s_mTps, b + 1)
                    if past(b):
                        act.wait_ge(s_shift, 32 * b)
                    act.activation(mT[:, :, :].rearrange("r n q -> r (n q)"),
                                   psV[0:2 * 3 * H, :].bitcast(bf16)[:, 0:T // 2], ACT.Copy).then_inc(s_mT, 1)
                if a is not None:
                    qk_high(a, 1)
                for step in range(STEPS):
                    s = step // SUB
                    if b is not None and step % SUB == 0:
                        exp(b, s)
                        if s % 8 == 2 and s > 8:
                            pv_copy(b, s // 8 - 1)
                    if a is not None and step in (0, SUB):
                        qk_high(a, 2 + s)
                    if c is not None:
                        if step == SUB * FFN_START - SUB:
                            ffn_high(c, 0)
                            ffn_high(c, 1)
                        for u in ffn_done(step - 1):
                            if u == 2 and a is not None:
                                act.wait_ge(s_stack[0], 96 * (a + 1))
                                act.wait_ge(s_stack[1], 96 * (a + 1))
                            ffn_high(c, u)
                if b is not None:
                    pv_copy(b, NG - 1)

            run(act, iteration)

        @block.vector
        def _(dve):
            def norm_stats(ln, row, src):
                for n in range(NT):
                    last = dve.bn_stats(ln.stats[:, n, :], src[:, n, :])
                last.then_inc(ln.s_stats, 1)
                dve.wait_ge(ln.s_stats, row + 1)
                dve.sem_inc(s_seen, 1)
                for n in range(NT):
                    last = dve.bn_aggr(ln.mv[:, n, :], ln.stats[:, n, :])
                last.then_inc(ln.s_mv, 1)
                dve.wait_ge(ln.s_mv, row + 1)
                dve.tensor_scalar(ln.ve[:, :], ln.mv[:, :, 1], EPS, None, ALU.add).then_inc(ln.s_ve, 1)

            def norm_apply(ln, row, dst, src):
                dve.wait_ge(ln.s_rstd, row + 1)
                for n in range(NT):
                    last = dve.tensor_scalar(dst[:, n, :], src[:, n, :], ln.mv[:, n, 0:1], ln.rstd[:, n:n + 1],
                                             ALU.subtract, ALU.mult)
                last.then_inc(ln.s_out, 1)

            dve.wait_ge(s_x, 16)
            dve.wait_ge(s_const, 1)
            norm_stats(ln1, 0, x_in)
            dve.memset(vv[0][:, :, :, :, 1].rearrange("p n h d -> p (n h) d"), 1.0)
            norm_apply(ln1, 0, x_in, x_in)
            dve.wait_ge(s_wraw, 16 * 2)
            for j in range(4):
                raw = (wq_raw, wk_raw)[j // 2]
                for k in range(KC):
                    last = dve.tensor_copy(
                        wqk[:, j, k, :].rearrange("p (d h) -> p d h", h=HT),
                        raw[:, k, (j % 2) * P:(j % 2 + 1) * P].rearrange("p (h d) -> p d h", d=D))
            last.then_inc(s_wqk, 1)
            dve.memset(vv[1][:, :, :, :, 1].rearrange("p n h d -> p (n h) d"), 1.0)
            dve.wait_ge(s_wts, 16 * 10)

            def signs():
                dve.wait_ge(s_scl, 16 * 3)
                steps = [0]

                def step(ins):
                    steps[0] += 1
                    ins.then_inc(s_sgs, 1)
                    dve.wait_ge(s_sgs, steps[0])

                step(dve.tensor_scalar(sc[:, 8:10], sc[:, 0:2], 0.0, None, ALU.is_gt))
                step(dve.tensor_scalar(sc[:, 10:12], sc[:, 0:2], 0.0, None, ALU.is_lt))
                step(dve.tensor_tensor(sc[:, 12:14], sc[:, 8:10], sc[:, 10:12], ALU.subtract))
                step(dve.tensor_scalar(sc[:, 3:4], sc[:, 12:13], 2.0, None, ALU.mult))
                step(dve.tensor_scalar(sc[:, 5:6], sc[:, 13:14], 2.0 * H2_SCALE, None, ALU.mult))
                dve.tensor_scalar(sc[:, 6:7], sc[:, 13:14], -H2_SCALE, None, ALU.mult).then_inc(s_sgn, 1)
                step(dve.tensor_tensor(sc[:, 14:16], sc[:, 0:2], sc[:, 12:14], ALU.mult))
                step(dve.tensor_tensor(sc[:, 8:9], sc[:, 14:15], sc[:, 15:16], ALU.mult))
                step(dve.tensor_tensor(sc[:, 9:10], sc[:, 8:9], sc[:, 2:3], ALU.mult))
                step(dve.tensor_scalar(sc[:, 7:8], sc[:, 9:10], 4.0 / H2_SCALE, None, ALU.mult))

            def w0_difference():
                dve.wait_ge(s_kraw, 16 * 3)
                for k in range(KC):
                    last = dve.tensor_tensor(w0[:, k, :], k0_raw[:, k, :], k0_raw[:, KC + k, :], ALU.subtract)
                last.then_inc(s_w0d, 1)
                dve.wait_ge(s_w0d, 1)
                dve.tensor_scalar(w0[:, :, :], w0[:, :, :], sc[:, 3:4], None, ALU.mult).then_inc(s_wffn, 1)

            def qk_parts(a, j):
                high, mid = (part[:, j % 2, :] for part in parts[j // 2][0:2])
                if past(a) or j >= 2:
                    dve.wait_ge(s_lo, 4 * a + j - 1)
                dve.wait_ge(s_hi, 4 * a + j + 1)
                dve.scalar_tensor_tensor(out=resid[j % 2][:, :], in0=psA[:, j % 2, :], scalar=bqk[:, j:j + 1],
                                         in1=high, op0=ALU.add, op1=ALU.subtract).then_inc(s_r1, 1)
                dve.wait_ge(s_r1, 4 * a + j + 1)
                dve.tensor_copy(mid, resid[j % 2][:, :]).then_inc(s_mid, 1)

            def v_copy(a, par, n):
                dve.wait_ge(s_vps, 2 * a + n + 1)
                for e in range(2):
                    last = dve.tensor_tensor(
                        vv[par][:, 2 * n + e, :, :, 0],
                        psA[:, n, e * C:(e + 1) * C].rearrange("p (h d) -> p h d", d=D),
                        bv_r.rearrange("p (h d) -> p h d", d=D), ALU.add)
                last.then_inc(s_v, 1)

            def unit_max(a, banks, u):
                h, at = u // len(QB), 0
                dve.wait_ge(s_s, NU * a + u + 1)
                dve.sem_inc(s_seen, 1)
                for qb in QB[u % len(QB)]:
                    n = (qb + 1) * P
                    sc_ = banks[u % len(banks)][:, at:at + n]
                    last = dve.tensor_tensor_reduce(out=sc_, in0=sc_, in1=causal[:, T - n:T], scale=1.0,
                                                    scalar=-3.0e38, op0=ALU.add, op1=ALU.max,
                                                    accum_out=rowmax[:, qb, h:h + 1])
                    at += n
                last.then_inc(s_max, 1)

            def max_parts(a):
                dve.wait_ge(s_max, NU * (a + 1))
                if past(a):
                    dve.wait_ge(s_mTps, a)
                part = [mparts[:, :, H * n:H * n + H] for n in range(3)]
                dve.tensor_scalar(part[0], rowmax[:, :, :], -1.0, None, ALU.mult).then_inc(s_mstep, 1)
                dve.wait_ge(s_mstep, 3 * a + 1)
                dve.scalar_tensor_tensor(out=negr[:, :, :], in0=rowmax[:, :, :], scalar=-1.0, in1=part[0],
                                         op0=ALU.mult, op1=ALU.subtract).then_inc(s_mstep, 1)
                dve.wait_ge(s_mstep, 3 * a + 2)
                dve.tensor_copy(part[1], negr[:, :, :]).then_inc(s_mstep, 1)
                dve.wait_ge(s_mstep, 3 * a + 3)
                dve.tensor_tensor(part[2], negr[:, :, :], part[1], ALU.subtract).then_inc(s_mparts, 1)

            def invert(b, t, n):
                if n == 0:
                    dve.wait_ge(s_pack[0], 16 * (2 * b + t + 1))
                    dve.wait_ge(s_pack[1], 16 * (2 * b + t + 1))
                part = sums[:, t, n * P:(n + 1) * P]
                dve.reciprocal(part, part).then_inc(s_rec, 1)

            def divide(b, t, first=0, last=NT - 1):
                dve.wait_ge(s_rec, (KC * b + t) * NT + last + 1)
                cols = slice(first * P, (last + 1) * P)
                dve.tensor_tensor(att[:, t, cols], att[:, t, cols], sums[:, t, cols], ALU.mult).then_inc(s_att, 1)

            def ffn_low(c, u):
                dve.wait_ge(s_ch, (NC_USES - 2) * c + u + 1)
                if u < 2:
                    dve.tensor_tensor(zT[1][:, u, :], c_bank(u), zT[0][:, u, :], ALU.subtract).then_inc(s_cl, 1)
                else:
                    h, m = (h1 if u < 2 + KF else h2), (u - 2) % KF
                    dve.scalar_tensor_tensor(out=h[1][:, m, :], in0=c_bank(u), scalar=0.0, in1=h[0][:, m, :],
                                             op0=ALU.max, op1=ALU.subtract).then_inc(s_cl, 1)

            def finish(c, par, n):
                u = NC_USES - 2 + n
                dve.wait_ge(s_c, NC_USES * c + u + 1)
                o = x1[par][:, 2 * n:2 * n + 2, :].rearrange("p n c -> p (n c)")
                dve.scalar_tensor_tensor(out=o, in0=c_bank(u), scalar=sc[:, 7:8], in1=o,
                                         op0=ALU.mult, op1=ALU.add).then_inc(s_cl, 1)

            def iteration(i, par, looped=False):
                a, b, c, cr, an = stages(i, looped)
                if a is not None:
                    qk_parts(a, 0)
                if cr is not None:
                    finish(cr, 1 - par, 0)
                if c is not None:
                    for n in range(2):
                        dve.wait_ge(s_wo, 2 * c + n + 1)
                        dve.tensor_tensor(y[:, 2 * n:2 * n + 2, :],
                                          psB[:, n, :].rearrange("p (n c) -> p n c", n=2),
                                          bo_r[:, None, :].to_broadcast([P, 2, C]), ALU.add).then_inc(s_y, 1)
                    dve.wait_ge(s_y, 2 * c + 2)
                    norm_stats(lny, c, y)
                if a is not None:
                    qk_parts(a, 1)
                if c is not None:
                    dve.wait_ge(lny.s_rstd, c + 1)
                    for n in range(NT):
                        last = dve.scalar_tensor_tensor(out=y[:, n, :], in0=y[:, n, :], scalar=lny.mv[:, n, 0:1],
                                                        in1=gamma_r, op0=ALU.subtract, op1=ALU.mult)
                    last.then_inc(s_yg, 1)
                    dve.wait_ge(s_yg, c + 1)
                    dve.wait_ge(s_xb, c + 1)
                    xr = x1[par]
                    for n in range(NT):
                        last = dve.scalar_tensor_tensor(out=xr[:, n, :], in0=y[:, n, :], scalar=lny.rstd[:, n:n + 1],
                                                        in1=xr[:, n, :], op0=ALU.mult, op1=ALU.add)
                    last.then_inc(s_x1, 1)
                    dve.wait_ge(s_x1, c + 1)
                    norm_stats(ln2, c, xr)
                if a is not None:
                    qk_parts(a, 2)
                if c is not None:
                    norm_apply(ln2, c, y, x1[par])
                if a is not None:
                    qk_parts(a, 3)
                if cr is not None:
                    finish(cr, 1 - par, 1)
                if c is not None:
                    ffn_low(c, 0)
                    ffn_low(c, 1)
                if a is not None:
                    v_copy(a, par, 0)
                    v_copy(a, par, 1)
                if not looped and i == 0:
                    signs()
                if not looped and i == 1:
                    w0_difference()
                for step in range(STEPS):
                    s = step // SUB
                    if a is not None:
                        for u in s_units(step):
                            unit_max(a, s_banks(c), u)
                    if c is not None:
                        for u in ffn_done(step - 2):
                            ffn_low(c, u)
                    if an is not None and step == SUB * 14:
                        dve.wait_ge(s_x, 16 * (an + 1))
                        norm_stats(ln1, an, x_in)
                    if an is not None and step == SUB * 18:
                        norm_apply(ln1, an, x_in, x_in)
                    if b is not None and step in range(SUB * 24, SUB * 28, SUB):
                        invert(b, 0, s - 24)
                    if b is not None and step == SUB * 28:
                        divide(b, 0)
                if a is not None:
                    max_parts(a)
                if b is not None:
                    for n in (0, 2):
                        invert(b, 1, n)
                        invert(b, 1, n + 1)
                        divide(b, 1, n, n + 1)

            run(dve, iteration)

        @block.tensor
        def _(pe):
            pe.wait_ge(s_const, 1)

            def x_transposed(a):
                pe.wait_ge(ln1.s_out, a + 1)
                if past(a):
                    pe.wait_ge(s_max, NU * a)
                for k in range(KC):
                    for n in range(NT):
                        last = pe.transpose(psA[:, k, n * P:(n + 1) * P], x_in[:, n, k * P:(k + 1) * P], ident[:, :])
                    last.then_inc(s_xT, 1)

            def qk(a, j):
                if j == 0:
                    pe.wait_ge(s_xnT, 2 * a + 2)
                if j == 0 and not past(a):
                    pe.wait_ge(s_wqk, 1)
                    pe.wait_ge(s_wts, 16 * 10)
                if j >= 2:
                    pe.wait_ge(s_r1, 4 * a + j - 1)
                for k in range(KC):
                    last = pe.matmul(psA[:, j % 2, :], wqk[:, j, k, :], xnT[:, k, :], start=(k == 0), stop=(k == KC - 1))
                last.then_inc(s_qk, 1)

            def v(a, n):
                pe.wait_ge(s_r1, 4 * a + 3 + n)
                for e in range(2):
                    t = 2 * n + e
                    for k in range(KC):
                        last = pe.matmul(psA[:, n, e * C:(e + 1) * C], xnT[:, k, t * P:(t + 1) * P], wv[:, k, :],
                                         start=(k == 0), stop=(k == KC - 1))
                last.then_inc(s_vps, 1)

            def scores(a, par, banks, u):
                h, at = u // len(QB), 0
                if u == 0:
                    pe.wait_ge(s_stack[0], 96 * (a + 1))
                    pe.wait_ge(s_stack[1], 96 * (a + 1))
                    pe.wait_ge(s_v, 2 * a + 2)
                if u >= len(banks):
                    pe.wait_ge(s_max, NU * a + u - len(banks) + 1)
                for qb in QB[u % len(QB)]:
                    n = (qb + 1) * P
                    last = pe.matmul(banks[u % len(banks)][:, at:at + n], qS[par][0:ROWS_QK, h, qb * P:(qb + 1) * P],
                                     kS[par][0:ROWS_QK, h, 0:n], start=True, stop=True)
                    at += n
                last.then_inc(s_s, 1)

            def max_transposed(b):
                pe.wait_ge(s_mparts, b + 1)
                if past(b):
                    pe.wait_ge(s_o, NG * b)
                o = psV[0:2 * 3 * H, :].bitcast(bf16)
                for n in range(NT // 2):
                    last = pe.transpose(o[:, n * P:(n + 1) * P],
                                        mparts[:, 2 * n:2 * n + 2, :].rearrange("q e m -> q (e m)"), identh[:, :])
                last.then_inc(s_mTps, 1)

            def scores_t(b, par, s):
                g, kb, pr = s // 8, (s % 8) // 2, s % 2
                if s == 0:
                    pe.wait_ge(s_shift, 32 * (b + 1))
                if s == 0 and not past(b):
                    pe.wait_ge(s_ones, 2)
                if past(b) or s > 0:
                    pe.wait_ge(s_exp, NS * b + s)
                if s == 0 and past(b):
                    pe.wait_ge(s_y, 2 * b)
                for e in range(2):
                    h = 4 * g + 2 * pr + e
                    last = pe.matmul(psB[:, e, 0:T - kb * P], kS[par][0:ROWS_SHIFT, place(h), kb * P:(kb + 1) * P],
                                     qS[par][0:ROWS_SHIFT, place(h), kb * P:T], start=True, stop=True)
                last.then_inc(s_st, 1)

            def pv(b, par, j):
                g, kb = j // NT, j % NT
                pe.wait_ge(s_tri, NS * b + 2 * j + 2)
                if kb == 0:
                    if g > 0:
                        pe.wait_ge(s_o, NG * b + g)
                    else:
                        pe.wait_ge(s_mT, b + 1)
                for i4 in range(4):
                    last = pe.matmul(psV[32 * i4:32 * i4 + 32, kb * P:T], vv[par][:, kb, 4 * g + i4].rearrange("p d e -> p (d e)"),
                                     probs[j % 2][:, i4, 0:T - kb * P], start=(kb == 0), stop=(kb == NT - 1))
                last.then_inc(s_pv, 1)

            def project(c, half):
                pe.wait_ge(s_att, 3 * c + 2 + half)
                pe.wait_ge(s_exp, NS * (c + 1))
                for n in (2 * half, 2 * half + 1):
                    for t in range(KC):
                        last = pe.matmul(psB[:, n // 2, (n % 2) * C:(n % 2 + 1) * C], att[:, t, n * P:(n + 1) * P],
                                         wo[:, t, :], start=(t == 0), stop=(t == KC - 1))
                    if n % 2:
                        last.then_inc(s_wo, 1)

            def c_free(c, u):
                if u > 2:
                    pe.wait_ge(s_cl, NC_USES * c + min(u, NC_USES - 2) - 2)
                elif past(c):
                    pe.wait_ge(s_cl, NC_USES * c - (u < 2))

            def z_transposed(c):
                pe.wait_ge(ln2.s_out, c + 1)
                for u in range(KC):
                    c_free(c, u)
                    for n in range(NT):
                        last = pe.transpose(c_bank(u)[:, n * P:(n + 1) * P], y[:, n, u * P:(u + 1) * P], ident[:, :])
                    last.then_inc(s_c, 1)

            def ffn_piece(c, piece):
                first = piece < KC * KF
                m, k = divmod(piece, KC) if first else divmod(piece - KC * KF, KF)
                w, act_in, k_last, u = (w0, zT, KC - 1, 2 + m) if first else (w1, h1, KF - 1, 2 + KF + m)
                if k == 0:
                    c_free(c, u)
                if piece == 0:
                    pe.wait_ge(s_cl, NC_USES * c + 2)
                if not first and m == 0:
                    pe.wait_ge(s_cl, NC_USES * c + 2 + k + 1)
                for part in range(2):
                    last = pe.matmul(c_bank(u), w[:, k, m * P:(m + 1) * P], act_in[part][:, k, :],
                                     start=(k == 0 and part == 0), stop=(k == k_last and part == 1))
                if k == k_last:
                    last.then_inc(s_c, 1)

            def ffn3(c, n, quarter):
                u = NC_USES - 2 + n
                if quarter == 0:
                    c_free(c, u)
                    pe.wait_ge(s_cl, NC_USES * c + 2 + 2 * KF)
                e = quarter // 2
                t = 2 * n + e
                for k in range(KF // 2 * (quarter % 2), KF // 2 * (quarter % 2 + 1)):
                    for part in range(2):
                        last = pe.matmul(c_bank(u)[:, e * C:(e + 1) * C], h2[part][:, k, t * P:(t + 1) * P],
                                         w2[:, k, :], start=(k == 0 and part == 0), stop=(k == KF - 1 and part == 1))
                if quarter == 3:
                    last.then_inc(s_c, 1)

            def iteration(i, par, looped=False):
                a, b, c, cr, an = stages(i, looped)
                if a is not None:
                    if not looped and a == 0:
                        x_transposed(a)
                    qk(a, 0)
                if b is not None:
                    max_transposed(b)
                if c is not None:
                    project(c, 0)
                    project(c, 1)
                if a is not None:
                    qk(a, 1)
                for step in range(STEPS):
                    s = step // SUB
                    if b is not None and step % SUB == 0:
                        scores_t(b, 1 - par, s)
                    if cr is not None and step % SUB == 0 and s < 4:
                        ffn3(cr, 1, s)
                    if a is not None and step in (0, SUB):
                        qk(a, 2 + s)
                    if b is not None and step % (2 * SUB) == SUB + 2 and s >= 3:
                        pv(b, 1 - par, (s - 3) // 2)
                    if a is not None and step == SUB * FFN_START - SUB:
                        v(a, 0)
                    if c is not None and step == SUB * FFN_START - SUB + 1:
                        if not looped and c == 0:
                            pe.wait_ge(s_wffn, 2)
                        z_transposed(c)
                    if a is not None and step == SUB * FFN_START - 1:
                        v(a, 1)
                    if a is not None:
                        for u in s_units(step):
                            scores(a, par, s_banks(c), u)
                    if c is not None:
                        for piece in ffn_pieces(step):
                            ffn_piece(c, piece)
                if b is not None:
                    pv(b, 1 - par, NS // 2 - 1)
                if c is not None:
                    for quarter in range(3):
                        ffn3(c, 0, quarter)
                if an is not None:
                    x_transposed(an)
                if c is not None:
                    ffn3(c, 0, 3)

            run(pe, iteration)


_INS = ["L0_attn_x", "L0_attn_Wq", "L0_attn_bq", "L0_attn_Wk", "L0_attn_bk", "L0_attn_Wv", "L0_attn_bv",
        "L0_attn_Wo", "L0_attn_bo", "L0_attn_gamma", "L0_attn_beta", "L0_ffn_k0", "L0_ffn_k1", "L0_ffn_k2",
        "L0_ffn_s0", "L0_ffn_s1", "L0_ffn_s2"]


def kernel(**inputs):
    import numpy as np
    import concourse.bacc as bacc
    from concourse.bass_utils import run_bass_kernel_spmd

    nc = bacc.Bacc("TRN2", target_bir_lowering=False, num_devices=1)
    arrays, args = {}, []
    for name in _INS:
        a = np.ascontiguousarray(inputs[name])
        a = a.reshape(a.shape or (1,))
        arrays[f"in_{name}"] = a
        args.append(nc.dram_tensor(f"in_{name}", a.shape, mybir.dt.from_np(a.dtype), kind="ExternalInput").ap())
    shape = tuple(inputs["L0_attn_x"].shape)
    args.append(nc.dram_tensor("out_0", shape, mybir.dt.float32, kind="ExternalOutput").ap())
    layer_kernel(nc, *args)
    r = run_bass_kernel_spmd(nc, [arrays], core_ids=[0])
    return r.results[0]["out_0"]
```
